# Optimizing a Trainium2 kernel written in Bass

```python
import numpy as np
import jax
import jax.numpy as jnp

def _softmax(x, axis=-1):
    return jax.nn.softmax(x, axis=axis)

def _gelu(x):
    return jax.nn.gelu(x, approximate=True)

def _silu(x):
    return jax.nn.silu(x)

def _sigmoid(x):
    return jax.nn.sigmoid(x)

def _layernorm(x, axis=-1, eps=1e-05):
    m = jnp.mean(x, axis=axis, keepdims=True)
    v = jnp.var(x, axis=axis, keepdims=True)
    return (x - m) / jnp.sqrt(v + eps)

def _scatter_add(tgt, idx, src, axis=0):
    return tgt.at[idx].add(src)

def _segment_sum(src, seg, n):
    return jax.ops.segment_sum(src, seg, n)
kernel_name = 'mk_recurrent_d1_jaxref_r8_b7b626'

def setup_inputs(seed: int=0):
    np.random.seed(seed)
    _w = jnp.asarray

    def _L0_attn_setup():
        import jax, jax.numpy as jnp
        import numpy as np
        D_MODEL, N_QUERY, N_HEAD = (128, 2, 8)
        D_HEAD = D_MODEL // (N_QUERY * N_HEAD)
        KV = D_HEAD * N_HEAD

        def _reference_tuple_inner(x, Wq, Wk, Wv, memory, memory_norm, memory_weight):
            B, S, _ = x.shape
            QH = N_QUERY * N_HEAD
            scale = 1.0 / jnp.sqrt(jnp.float32(D_HEAD))
            q = x @ Wq
            k = x @ Wk
            v = x @ Wv
            q4 = q.reshape(B, S, QH, D_HEAD)
            k4 = jnp.repeat(k.reshape(B, S, N_HEAD, D_HEAD), N_QUERY, axis=2)
            v4 = jnp.repeat(v.reshape(B, S, N_HEAD, D_HEAD), N_QUERY, axis=2)
            scores = jnp.einsum('bsnd,btnd->bnst', q4, k4) * scale
            probs = jax.nn.softmax(scores, axis=-1)
            a_dot = jnp.einsum('bnst,btnd->bsnd', probs, v4)
            sigma_q = jax.nn.elu(q.reshape(B, S, N_QUERY, KV))
            num = sigma_q @ memory
            den = (sigma_q @ memory_norm)[..., None]
            a_mem = (num / den).reshape(B, S, QH, D_HEAD)
            sigma_k = jax.nn.elu(k)
            retrieved = sigma_k @ memory / (sigma_k @ memory_norm)[..., None]
            new_memory = memory + jnp.einsum('bsk,bsv->kv', sigma_k, v - retrieved)
            new_memory_norm = memory_norm + jnp.sum(sigma_k, axis=(0, 1))
            w = jax.nn.sigmoid(memory_weight)
            out = (a_dot * (1.0 - w) + a_mem * w).reshape(B, S, D_MODEL)
            return (out, new_memory, new_memory_norm)
        key = jax.random.key(seed)
        ks = jax.random.split(key, 6)
        B, S = (2, 256)
        x = jax.random.normal(ks[0], (B, S, D_MODEL), jnp.float32)
        Wq = jax.random.normal(ks[1], (D_MODEL, D_MODEL), jnp.float32) / np.sqrt(D_MODEL)
        Wk = jax.random.normal(ks[2], (D_MODEL, KV), jnp.float32) / np.sqrt(D_MODEL)
        Wv = jax.random.normal(ks[3], (D_MODEL, KV), jnp.float32) / np.sqrt(D_MODEL)
        memory = jax.random.normal(ks[4], (KV, KV), jnp.float32)
        memory_norm = jnp.ones((KV,), jnp.float32)
        memory_weight = jnp.ones((1,), jnp.float32)
        return {'x': x, 'Wq': Wq, 'Wk': Wk, 'Wv': Wv, 'memory': memory, 'memory_norm': memory_norm, 'memory_weight': memory_weight}
    _L0_attn_in = _L0_attn_setup()

    def _L0_ffn_setup():
        import jax, jax.numpy as jnp
        import numpy as np
        TOP_K = 2
        key = jax.random.key(seed)
        ks = jax.random.split(key, 6)
        B, T, H, E, F = (2, 256, 128, 8, 512)
        s = 0.02
        return {'hidden_states': jax.random.normal(ks[0], (B, T, H), dtype=jnp.float32), 'router_w': jax.random.normal(ks[1], (E, H), dtype=jnp.float32) * s, 'w1': jax.random.normal(ks[2], (E, F, H), dtype=jnp.float32) * s, 'b1': jax.random.normal(ks[3], (E, F), dtype=jnp.float32) * s, 'w2': jax.random.normal(ks[4], (E, H, F), dtype=jnp.float32) * s, 'b2': jax.random.normal(ks[5], (E, H), dtype=jnp.float32) * s}
    _L0_ffn_in = _L0_ffn_setup()
    _d = {'L0_attn_x': _L0_attn_in['x'], 'L0_attn_Wq': _L0_attn_in['Wq'], 'L0_attn_Wk': _L0_attn_in['Wk'], 'L0_attn_Wv': _L0_attn_in['Wv'], 'L0_attn_memory': _L0_attn_in['memory'], 'L0_attn_memory_norm': _L0_attn_in['memory_norm'], 'L0_attn_memory_weight': _L0_attn_in['memory_weight'], 'L0_ffn_router_w': _L0_ffn_in['router_w'], 'L0_ffn_w1': _L0_ffn_in['w1'], 'L0_ffn_b1': _L0_ffn_in['b1'], 'L0_ffn_w2': _L0_ffn_in['w2'], 'L0_ffn_b2': _L0_ffn_in['b2']}
    _x0 = _d['L0_attn_x']
    _d['L0_attn_x'] = jax.random.normal(jax.random.fold_in(jax.random.key(seed), 1), (8, 512, 128), dtype=_x0.dtype)
    del _x0
    return _d

def reference(L0_attn_x, L0_attn_Wq, L0_attn_Wk, L0_attn_Wv, L0_attn_memory, L0_attn_memory_norm, L0_attn_memory_weight, L0_ffn_router_w, L0_ffn_w1, L0_ffn_b1, L0_ffn_w2, L0_ffn_b2):

    def _L0_attn_ref(x, Wq, Wk, Wv, memory, memory_norm, memory_weight):
        import jax, jax.numpy as jnp
        import numpy as np
        D_MODEL, N_QUERY, N_HEAD = (128, 2, 8)
        D_HEAD = D_MODEL // (N_QUERY * N_HEAD)
        KV = D_HEAD * N_HEAD

        def _reference_tuple_inner(x, Wq, Wk, Wv, memory, memory_norm, memory_weight):
            B, S, _ = x.shape
            QH = N_QUERY * N_HEAD
            scale = 1.0 / jnp.sqrt(jnp.float32(D_HEAD))
            q = x @ Wq
            k = x @ Wk
            v = x @ Wv
            q4 = q.reshape(B, S, QH, D_HEAD)
            k4 = jnp.repeat(k.reshape(B, S, N_HEAD, D_HEAD), N_QUERY, axis=2)
            v4 = jnp.repeat(v.reshape(B, S, N_HEAD, D_HEAD), N_QUERY, axis=2)
            scores = jnp.einsum('bsnd,btnd->bnst', q4, k4) * scale
            probs = jax.nn.softmax(scores, axis=-1)
            a_dot = jnp.einsum('bnst,btnd->bsnd', probs, v4)
            sigma_q = jax.nn.elu(q.reshape(B, S, N_QUERY, KV))
            num = sigma_q @ memory
            den = (sigma_q @ memory_norm)[..., None]
            a_mem = (num / den).reshape(B, S, QH, D_HEAD)
            sigma_k = jax.nn.elu(k)
            retrieved = sigma_k @ memory / (sigma_k @ memory_norm)[..., None]
            new_memory = memory + jnp.einsum('bsk,bsv->kv', sigma_k, v - retrieved)
            new_memory_norm = memory_norm + jnp.sum(sigma_k, axis=(0, 1))
            w = jax.nn.sigmoid(memory_weight)
            out = (a_dot * (1.0 - w) + a_mem * w).reshape(B, S, D_MODEL)
            return (out, new_memory, new_memory_norm)
        return _reference_tuple_inner(x, Wq, Wk, Wv, memory, memory_norm, memory_weight)[0]

    def _L0_ffn_ref(hidden_states, router_w, w1, b1, w2, b2):
        import jax, jax.numpy as jnp
        import numpy as np
        TOP_K = 2
        x = hidden_states
        router_logits = jnp.einsum('bth,eh->bte', x, router_w)
        topk_values, topk_indices = jax.lax.top_k(router_logits, TOP_K)
        topk_weights = jax.nn.softmax(topk_values.astype(jnp.float32), axis=-1).astype(x.dtype)
        h1 = jnp.einsum('bth,efh->btef', x, w1) + b1
        h1 = jax.nn.gelu(h1, approximate=False)
        expert_outputs = jnp.einsum('btef,ehf->bteh', h1, w2) + b2
        gather_idx = topk_indices[..., None]
        topk_expert_outputs = jnp.take_along_axis(expert_outputs, gather_idx, axis=2)
        mixed_output = jnp.sum(topk_expert_outputs * topk_weights[..., None], axis=2)
        return mixed_output
    x = L0_attn_x
    xn = _layernorm(x, axis=-1)
    s = _L0_attn_ref(xn, L0_attn_Wq, L0_attn_Wk, L0_attn_Wv, L0_attn_memory, L0_attn_memory_norm, L0_attn_memory_weight)
    g = _silu(_L0_ffn_ref(xn, L0_ffn_router_w, L0_ffn_w1, L0_ffn_b1, L0_ffn_w2, L0_ffn_b2))
    x = x + s * g
    return x

_drawn_inputs = setup_inputs


def setup_inputs(seed=0):
    import zlib

    import numpy as np

    out = dict(_drawn_inputs(seed))
    spreads = {'L0_attn_memory_norm': (1.0, 0.2)}
    factors = {'L0_attn_Wk': 8.0, 'L0_attn_Wv': 8.0}
    for name, (base, spread) in spreads.items():
        noise = np.random.default_rng([zlib.crc32(name.encode()), seed]).standard_normal(out[name].shape)
        drawn = base * np.exp(spread * noise) if base else spread * noise
        out[name] = jnp.asarray(drawn.astype(out[name].dtype))
    for name, factor in factors.items():
        out[name] = (out[name] * factor).astype(out[name].dtype)
    return out
```

```python
from contextlib import ExitStack

import numpy as np

import concourse.bass as bass
from concourse import mybir

F32 = mybir.dt.float32
F32R = mybir.dt.float32r
U32 = mybir.dt.uint32
ALU = mybir.AluOpType
ACT = mybir.ActivationFunctionType
AX = mybir.AxisListType

P = 128
BATCH, SEQ, DM = 8, 512, 128
HEADS, DH, KVH = 16, 8, 8
TILES = BATCH * SEQ // P
TPB = SEQ // P
GROUPS = 4
UNITS = BATCH * GROUPS
EXPERTS, FF = 8, 512
FT = FF // P
VW = DH + 1
VCOLS = KVH * VW
MEMW = 65
LN_EPS = 1e-5
SCALE = 1.0 / float(np.sqrt(DH))


STEPS = UNITS + 3


def front_loop(eng, step):
    for b in range(2):
        step(b, b)
    with eng.Fori(0, (BATCH - 2) // 2) as i:
        for s in (2, 3):
            step(s, i * 2 + s)


def unit_loop(eng, step):
    last = 4 + (UNITS - 4) // 4 * 4 - 4
    for t in range(4):
        step(t, t, lambda k: (t + k) // 4, lambda k: (t + k) // 2)
    with eng.Fori(0, (last - 4) // 4) as i:
        for s in range(4, 8):
            step(s, i * 4 + s, lambda k: i + (s + k) // 4, lambda k: i * 2 + (s + k) // 2)
    for t in range(last, STEPS):
        step(t, t, lambda k: (t + k) // 4, lambda k: (t + k) // 2)


def build(nc, x, wq_stack, wk_stack, wq, wv_router, mem_block, mem_weight, w1, b1, w2, b2, ident_in,
          sign_rows, ones_rows, iota_in, out):
    ctx = ExitStack()
    with ctx:
        def sb(name, shape, dt=F32):
            return ctx.enter_context(nc.sbuf_tensor(name, shape, dt))

        def sem(name):
            return ctx.enter_context(nc.semaphore(name))

        xs = sb("xs", [P, TILES, DM])
        xn = sb("xn", [P, TILES, DM])
        xnT = sb("xnT", [P, BATCH * SEQ])
        att = sb("att", [P, TILES, DM])
        amem = sb("amem", [P, TILES, DM])
        values = sb("values", [P, TILES, VCOLS])
        logits = sb("logits", [P, TILES, EXPERTS])
        ident = sb("ident", [P, P])
        wqs = sb("wqs", [P, GROUPS, P])
        wks = sb("wks", [P, GROUPS, P])
        wqp = sb("wqp", [P, DM])
        wvr = sb("wvr", [P, VCOLS + EXPERTS])
        memb = sb("memb", [P, 2 * MEMW])
        consts = sb("consts", [P, 3])
        q_sign, k_sign, k_ones = consts[:, 0:1], consts[:, 1:2], consts[:, 2:3]
        mw = sb("mw", [P, 1])
        tanh_w = sb("tanh_w", [P, 1])
        w_mem = sb("w_mem", [P, 1])
        w_dot = sb("w_dot", [P, 1])
        eps = sb("eps", [P, 1])
        stats = sb("stats", [P, TILES, 6])
        mv = sb("mv", [P, TILES, 2])
        std = sb("std", [P, TILES])
        rstd = sb("rstd", [P, TILES])
        front_buf = sb("front_buf", [P, EXPERTS, SEQ])
        xT = front_buf[:, 0:2, :]
        q_neg, q_pos, q_exp, q_tanh, sigma = (front_buf[:, 2 + k, :] for k in range(5))
        mden = sb("mden", [P, TPB, 2])
        mden_w = sb("mden_w", [P, TPB, 2])
        q_hi = sb("q_hi", [P, SEQ], F32R)
        k_hi = sb("k_hi", [P, SEQ], F32R)
        q_stack = sb("q_stack", [P, 4, SEQ], F32R)
        k_stack = sb("k_stack", [P, 2, SEQ], F32R)
        k_zero = sb("k_zero", [P, 4, 4, SEQ], F32R)
        v_unit = sb("v_unit", [P, 4, TPB, 2 * VW + 23])
        neg_max = sb("neg_max", [P, 2, 16])
        m_hi = sb("m_hi", [16, P], F32R)
        m_lo = sb("m_lo", [16, P], F32R)
        probs = sb("probs", [P, 8, SEQ])
        pv_sb = sb("pv_sb", [P, SEQ])
        rden = sb("rden", [P, TPB, 4])
        w1s = sb("w1s", [P, EXPERTS, FF])
        b1s = sb("b1s", [P, EXPERTS, FT])
        b2s = sb("b2s", [1, EXPERTS, DM])
        one_row = sb("one_row", [1, P])
        iota = sb("iota", [P, EXPERTS])
        top = sb("top", [P, TILES, 8])
        top_i = sb("top_i", [P, TILES, 8], U32)
        top_f = sb("top_f", [P, TILES, 2])
        gap = sb("gap", [P, TILES])
        tgap = sb("tgap", [P, TILES])
        gates = sb("gates", [P, 2, TILES])
        coef = sb("coef", [P, TILES, EXPERTS])
        coef2 = top
        w2s = front_buf[:].rearrange("p e (f d) -> p e f d", d=DM)
        hidden = probs
        acc = xn

        ps = ctx.enter_context(nc.psum_tensor("ps", [P, 8, SEQ], F32))

        in_w, in_ffn = sem("in_w"), sem("in_ffn")
        in_x = [sem(f"in_x{b}") for b in range(BATCH)]
        setup = sem("setup")
        chain = sem("chain")
        chain2, mchain, rchain, fchain = sem("chain2"), sem("mchain"), sem("rchain"), sem("fchain")
        var_ready, std_ready = sem("var_ready"), sem("std_ready")
        xn_ready = sem("xn_ready")
        mw_ready = sem("mw_ready")
        xT_psum, xT_ready, xnT_ready = sem("xT_psum"), sem("xT_ready"), sem("xnT_ready")
        vr_psum, vr_used = sem("vr_psum"), sem("vr_used")
        q_psum, q_neg_ready, q_et_ready, sigma_ready = sem("q_psum"), sem("q_neg_ready"), sem("q_et_ready"), sem("sigma_ready")
        mem_psum, mem_used = sem("mem_psum"), sem("mem_used")
        ka_psum, k_hi_ready, ks_ready, kz_ready = sem("ka_psum"), sem("k_hi_ready"), sem("ks_ready"), [sem("kz_ready0"), sem("kz_ready1")]
        qa_psum, q_hi_ready, qs_ready = sem("qa_psum"), sem("q_hi_ready"), sem("qs_ready")
        s_psum, max_ready = sem("s_psum"), sem("max_ready")
        mt_psum, m_hi_ready, m_ready, m_rows = sem("mt_psum"), sem("m_hi_ready"), sem("m_ready"), sem("m_rows")
        st_psum, p_ready = sem("st_psum"), sem("p_ready")
        v_ready = sem("v_ready")
        pv_psum, pv_copied = sem("pv_psum"), sem("pv_copied")
        o_psum, rden_ready, att_ready = sem("o_psum"), sem("rden_ready"), sem("att_ready")
        h_psum, h_ready, y_psum, y_used = sem("h_psum"), sem("h_ready"), sem("y_psum"), sem("y_used")
        gap_ready, tgap_ready = sem("gap_ready"), sem("tgap_ready")
        acc_ready, silu_ready, fin_ready, stored = sem("acc_ready"), sem("silu_ready"), sem("fin_ready"), sem("stored")

        block = ctx.enter_context(nc.Block())

        x_view = x.rearrange("b (q p) d -> p b q d", p=P)
        out_view = out.rearrange("b (q p) d -> p b q d", p=P)

        def in_range(u):
            return 0 <= u < UNITS

        @block.sync
        def _(sp):
            for b in range(BATCH):
                sp.dma_start(xs[:, b * TPB:(b + 1) * TPB, :], x_view[:, b]).then_inc(in_x[b], 16)
                if b == 0:
                    for dst, src in ((ident[:], ident_in), (wqp[:], wq), (wvr[:], wv_router), (memb[:], mem_block),
                                     (consts[:, 0:2], sign_rows), (consts[:, 2:3], ones_rows),
                                     (mw[:], mem_weight.partition_broadcast(P)), (wqs[:], wq_stack), (wks[:], wk_stack),
                                     (iota[:], iota_in)):
                        sp.dma_start(dst, src).then_inc(in_w, 16)
            for dst, src in ((w1s[:], w1), (b1s[:], b1), (b2s[:], b2)):
                sp.dma_start(dst, src).then_inc(in_ffn, 16)
            sp.wait_ge(setup, 1)

            def place_keys(st):
                for j in range(4):
                    r = slice(32 * j, 32 * j + 32)
                    sp.dma_start(k_zero[r, st % 4, j, :].bitcast(F32),
                                 k_stack[r, st % 2, :].bitcast(F32)).then_inc(kz_ready[st % 2], 16)

            def step(st, t, batch, half):
                if in_range(st - 1):
                    sp.wait_ge(m_ready, t)
                    for row, part in ((24, m_hi), (25, m_lo)):
                        sp.dma_start(q_stack[row:P:32, (st - 1) % 4, :].bitcast(F32),
                                     part[:].bitcast(F32)).then_inc(m_rows, 16)
                if in_range(st + 1):
                    sp.wait_ge(ks_ready, t + 2)
                    place_keys(st + 1)
            sp.wait_ge(ks_ready, 1)
            place_keys(0)
            unit_loop(sp, step)
            sp.wait_ge(mem_used, BATCH)
            sp.dma_start(w2s, w2).then_inc(in_ffn, 16)

            for b in range(BATCH):
                sp.wait_ge(fin_ready, b + 1)
                sp.dma_start(out_view[:, b], xs[:, b * TPB:(b + 1) * TPB, :]).then_inc(stored, 16)
            sp.wait_ge(stored, 16 * BATCH)

        @block.gpsimd
        def _(pool):
            pool.memset(k_zero[:].bitcast(F32), 0.0).then_inc(setup, 1)
            pool.memset(values[:], 1.0).then_inc(setup, 1)
            pool.memset(v_unit[:], 0.0).then_inc(setup, 1)
            pool.wait_ge(setup, 3)
            pool.wait_ge(vr_used, 2 * BATCH)

            for g in range(4):
                pool.tensor_copy(v_unit[:, g, :, 0:2 * VW],
                                 values[:, 0:TPB, 2 * VW * g:2 * VW * (g + 1)]).then_inc(v_ready, 1)
            with pool.Fori(1, BATCH) as b:
                for g in range(4):
                    pool.wait_ge(pv_psum, (b * 4 + (g - 3)) * TPB)
                    pool.tensor_copy(v_unit[:, g, :, 0:2 * VW],
                                     values[:, bass.ts(b, TPB), 2 * VW * g:2 * VW * (g + 1)]).then_inc(v_ready, 1)

        @block.scalar
        def _(act):
            act.wait_ge(var_ready, 1)
            nc.scalar.activation(std[:], mv[:, :, 1], ACT.Sqrt, bias=eps[:]).then_inc(std_ready, 1)
            act.wait_ge(in_w, 160)
            nc.scalar.activation(tanh_w[:], mw[:], ACT.Tanh, scale=0.5).then_inc(mw_ready, 1)

            def front(st, b):
                act.wait_ge(xT_psum, b + 1)
                act.wait_ge(xT_ready, b + 1)
                nc.scalar.copy(xnT[:, bass.ts(b, SEQ)], ps[:, st % 2, :]).then_inc(xnT_ready, 1)
                act.wait_ge(q_neg_ready, 2 * b + 2)
                if st >= 1:
                    act.wait_ge(sigma_ready, b)
                nc.scalar.activation(q_exp, q_neg, ACT.Exp).then_inc(q_et_ready, 1)
                nc.scalar.activation(q_tanh, q_neg, ACT.Tanh, scale=0.5).then_inc(q_et_ready, 1)
            front_loop(act, front)

            def exp_chunk(st, u, c, js):
                for j in js:
                    k = u * 16 + (4 * c + j)
                    act.wait_ge(st_psum, k + 1)
                    n = 4 * c + j
                    if j == 0 and (st >= 1 or c >= 2):
                        act.wait_ge(pv_psum, u * 4 + (c - 1))
                    nc.scalar.activation(probs[:, n % 8, :], ps[:, 4 + n % 2, :], ACT.Exp, scale=SCALE).then_inc(p_ready, 1)

            def step(st, t, batch, half):
                c_on, o_on = in_range(st - 2), in_range(st - 3)
                for c in range(4):
                    if c_on:
                        exp_chunk(st - 2, t - 2, c, (0, 1))
                    if c == 0 and in_range(st + 1):
                        u = t + 1
                        act.wait_ge(ka_psum, u + 1)
                        act.wait_ge(ks_ready, u)
                        nc.scalar.activation(k_hi[:], ps[:, 7, :], ACT.Identity, bias=k_ones).then_inc(k_hi_ready, 1)
                    if c == 1 and o_on:
                        u = t - 3
                        act.wait_ge(pv_psum, (u + 1) * 4)
                        if st - 3 >= 1:
                            act.wait_ge(o_psum, u)
                        nc.scalar.copy(pv_sb[:], ps[:, 6, :]).then_inc(pv_copied, 1)
                    if c_on:
                        exp_chunk(st - 2, t - 2, c, (2, 3))
                    if c == 1 and in_range(st + 1):
                        u = t + 1
                        act.wait_ge(qa_psum, u + 1)
                        act.wait_ge(qs_ready, u)
                        nc.scalar.copy(q_hi[:], ps[:, 7, :]).then_inc(q_hi_ready, 1)
            act.wait_ge(ka_psum, 1)
            nc.scalar.activation(k_hi[:], ps[:, 7, :], ACT.Identity, bias=k_ones).then_inc(k_hi_ready, 1)
            act.wait_ge(qa_psum, 1)
            nc.scalar.copy(q_hi[:], ps[:, 7, :]).then_inc(q_hi_ready, 1)
            unit_loop(act, step)

            act.wait_ge(gap_ready, 1)
            nc.scalar.activation(tgap[:], gap[:], ACT.Tanh, scale=0.5).then_inc(tgap_ready, 1)

            with act.Fori(0, BATCH) as b:
                for e in range(EXPERTS):
                    for f in range(FT):
                        k = b * (EXPERTS * FT) + (e * FT + f)
                        act.wait_ge(h_psum, k + 1)
                        if e >= 2:
                            act.wait_ge(y_psum, b * EXPERTS + (e - 1))
                        elif f == 0:
                            act.wait_ge(y_psum, b * EXPERTS)
                        nc.scalar.activation(hidden[:, 4 * (e % 2) + f, :], ps[:, f, :], ACT.Gelu,
                                             bias=b1s[:, e, f:f + 1]).then_inc(h_ready, 1)
            for b in range(BATCH):
                act.wait_ge(acc_ready, 1)
                nc.scalar.activation(acc[:, b * TPB:(b + 1) * TPB, :], acc[:, b * TPB:(b + 1) * TPB, :],
                                     ACT.Silu).then_inc(silu_ready, 1)

        @block.vector
        def _(dve):
            V = nc.vector
            V.memset(eps[:], LN_EPS)
            V.memset(one_row[:], 1.0)
            for b in range(BATCH):
                dve.wait_ge(in_x[b], 16)
                for t in range(b * TPB, (b + 1) * TPB):
                    V.bn_stats(stats[:, t, :], xs[:, t, :]).then_inc(chain, 1)
            dve.wait_ge(chain, TILES)
            for t in range(TILES):
                ins = V.bn_aggr(mv[:, t, :], stats[:, t, :])
            ins.then_inc(var_ready, 1)
            dve.wait_ge(std_ready, 1)
            V.reciprocal(rstd[:], std[:]).then_inc(chain, 1)
            dve.wait_ge(chain, TILES + 1)
            for t in range(TILES):
                ins = V.tensor_scalar(xn[:, t, :], xs[:, t, :], mv[:, t, 0:1], rstd[:, t:t + 1],
                                      ALU.subtract, ALU.mult)
                if t % TPB == TPB - 1:
                    ins.then_inc(xn_ready, 1)
            dve.wait_ge(mw_ready, 1)
            V.tensor_scalar(w_mem[:], tanh_w[:], 0.5, 0.5, ALU.mult, ALU.add).then_inc(chain, 1)
            V.tensor_scalar(w_dot[:], tanh_w[:], -0.5, 0.5, ALU.mult, ALU.add).then_inc(chain, 1)
            dve.wait_ge(chain, TILES + 3)
            dve.wait_ge(setup, 3)

            def front(st, b):
                dve.wait_ge(xT_psum, b + 1)
                if st >= 2:
                    dve.wait_ge(vr_psum, b - 1)
                V.tensor_copy(xT[:, st % 2, :], ps[:, st % 2, :]).then_inc(xT_ready, 1)
                dve.wait_ge(q_psum, b + 1)
                if st >= 1:
                    dve.wait_ge(q_et_ready, 2 * b)
                V.tensor_scalar(q_neg, ps[:, 3, :], 0.0, None, ALU.min).then_inc(q_neg_ready, 1)
                V.tensor_scalar(q_pos, ps[:, 3, :], 0.0, None, ALU.max).then_inc(q_neg_ready, 1)
                dve.wait_ge(vr_psum, b + 1)
                vr = ps[:, 2, 0:TPB * 80].rearrange("p (t c) -> p t c", t=TPB)
                for q in range(TPB):
                    ins = V.tensor_scalar(values[:, bass.ts(b * TPB + q, 1), :].rearrange("p a (h c) -> p (a h) c", c=VW)[:, :, 0:DH],
                                    vr[:, q, 0:VCOLS].rearrange("p (h c) -> p h c", c=VW)[:, :, 0:DH],
                                    w_dot[:], None, ALU.mult)
                ins.then_inc(vr_used, 1)
                V.tensor_copy(logits[:, bass.ts(b, TPB), :], vr[:, :, VCOLS:VCOLS + EXPERTS]).then_inc(vr_used, 1)
                dve.wait_ge(q_et_ready, 2 * b + 2)
                dve.wait_ge(q_neg_ready, 2 * b + 2)
                if st >= 1:
                    dve.wait_ge(mem_psum, b)
                V.scalar_tensor_tensor(out=q_exp, in0=q_exp, scalar=1.0, in1=q_tanh,
                                       op0=ALU.add, op1=ALU.mult).then_inc(chain2, 1)
                dve.wait_ge(chain2, b + 1)
                V.tensor_tensor(sigma, q_exp, q_pos, ALU.add).then_inc(sigma_ready, 1)
                dve.wait_ge(mem_psum, b + 1)
                num = ps[:, 4:6, :].rearrange("p a (c n) -> p (a c) n", c=2)
                V.reciprocal(mden[:], num[:, :, MEMW - 1:2 * MEMW:MEMW]).then_inc(mchain, 1)
                dve.wait_ge(mchain, 2 * b + 1)
                V.tensor_scalar(mden_w[:], mden[:], w_mem[:], None, ALU.mult).then_inc(mchain, 1)
                dve.wait_ge(mchain, 2 * b + 2)
                for g in range(2):
                    ins = V.tensor_tensor(amem[:, bass.ts(b, TPB), 64 * g:64 * g + 64],
                                          num[:, :, MEMW * g:MEMW * g + 64],
                                          mden_w[:, :, g:g + 1].to_broadcast([P, TPB, 64]), ALU.mult)
                ins.then_inc(mem_used, 1)
            front_loop(dve, front)

            def stack(hi, sign, dst, ready):
                return V.scalar_tensor_tensor(out=dst, in0=hi.bitcast(F32), scalar=sign, in1=ps[:, 7, :],
                                              op0=ALU.mult, op1=ALU.add).then_inc(ready, 1)

            def maxima(st, t, c):
                for h in range(2):
                    dve.wait_ge(s_psum, t * 8 + (2 * c + h + 1))
                    if c == 0 and h == 0 and st >= 2:
                        dve.wait_ge(mt_psum, t - 1)
                    V.tensor_reduce(neg_max[:, st % 2, 8 * h + c:8 * h + c + 5:4], ps[:, 2 * h:2 * h + 2, :],
                                    AX.X, ALU.max, negate=True).then_inc(max_ready, 1)

            def step(st, t, batch, half):
                if in_range(st - 1):
                    u = t - 1
                    dve.wait_ge(mt_psum, u + 1)
                    if st - 1 >= 1:
                        dve.wait_ge(m_rows, 32 * u)
                    V.tensor_copy(m_hi[:], ps[0:16, 7, 0:P]).then_inc(m_hi_ready, 1)
                    dve.wait_ge(m_hi_ready, u + 1)
                    V.tensor_tensor(m_lo[:], ps[0:16, 7, 0:P], m_hi[:].bitcast(F32), ALU.subtract).then_inc(m_ready, 1)
                for c in range(4):
                    if in_range(st):
                        maxima(st, t, c)
                    if c == 0 and in_range(st + 1):
                        u = t + 1
                        dve.wait_ge(k_hi_ready, u + 1)
                        if st + 1 >= 2:
                            dve.wait_ge(kz_ready[(st + 1) % 2], half(1) * 64)
                        if st + 1 >= 4:
                            dve.wait_ge(st_psum, (u - 3) * 16)
                        stack(k_hi[:], k_sign, k_stack[:, (st + 1) % 2, :], ks_ready)
                    if c == 1 and in_range(st + 1):
                        u = t + 1
                        dve.wait_ge(q_hi_ready, u + 1)
                        if st + 1 >= 4:
                            dve.wait_ge(st_psum, (u - 3) * 16)
                        stack(q_hi[:], q_sign, q_stack[:, (st + 1) % 4, :], qs_ready)
                    if c == 3 and in_range(st - 3):
                        u = t - 3
                        dve.wait_ge(o_psum, u + 1)
                        o = ps[:, 7, :].rearrange("p (t j d) -> p t j d", t=TPB, j=4)
                        V.reciprocal(rden[:], o[:, :, :, DH]).then_inc(rden_ready, 1)
                        dve.wait_ge(rden_ready, u + 1)
                        g, b = (st - 3) % 4, batch(-3)
                        for q in range(TPB):
                            ins = V.tensor_tensor(
                                att[:, bass.ts(b * TPB + q, 1), 32 * g:32 * g + 32].rearrange("p a (j d) -> p (a j) d", d=DH),
                                o[:, q, :, 0:DH], rden[:, q, :].unsqueeze(2).to_broadcast([P, 4, DH]), ALU.mult)
                        ins.then_inc(att_ready, 1)
            dve.wait_ge(k_hi_ready, 1)
            stack(k_hi[:], k_sign, k_stack[:, 0, :], ks_ready)
            dve.wait_ge(q_hi_ready, 1)
            stack(q_hi[:], q_sign, q_stack[:, 0, :], qs_ready)
            unit_loop(dve, step)

            n = 0
            for t in range(TILES):
                V.max(top[:, t, :], logits[:, t, :]).then_inc(rchain, 1)
            dve.wait_ge(rchain, TILES)
            for t in range(TILES):
                V.max_index(top_i[:, t, :], top[:, t, :], logits[:, t, :]).then_inc(rchain, 1)
            V.tensor_tensor(gap[:], top[:, :, 0], top[:, :, 1], ALU.subtract).then_inc(gap_ready, 1)
            dve.wait_ge(rchain, 2 * TILES)
            V.tensor_copy(top_f[:], top_i[:, :, 0:2]).then_inc(rchain, 1)
            dve.wait_ge(tgap_ready, 1)
            V.tensor_scalar(gates[:, 0, :], tgap[:], 0.5, 0.5, ALU.mult, ALU.add).then_inc(rchain, 1)
            V.tensor_scalar(gates[:, 1, :], tgap[:], -0.5, 0.5, ALU.mult, ALU.add).then_inc(rchain, 1)
            dve.wait_ge(rchain, 2 * TILES + 3)
            full = [P, TILES, EXPERTS]
            for k, dst in ((0, coef), (1, coef2)):
                V.tensor_tensor(dst[:], iota[:].unsqueeze(1).to_broadcast(full), top_f[:, :, k:k + 1].to_broadcast(full),
                                ALU.is_equal).then_inc(rchain, 1)
            dve.wait_ge(rchain, 2 * TILES + 5)
            for k, dst in ((0, coef), (1, coef2)):
                V.tensor_tensor(dst[:], dst[:], gates[:, k, :].unsqueeze(2).to_broadcast(full), ALU.mult).then_inc(rchain, 1)
            dve.wait_ge(rchain, 2 * TILES + 7)
            V.tensor_tensor(coef[:], coef[:], coef2[:], ALU.add).then_inc(rchain, 1)
            V.memset(acc[:], 0.0).then_inc(rchain, 1)
            dve.wait_ge(rchain, 2 * TILES + 9)

            with dve.Fori(0, BATCH) as b:
                for e in range(EXPERTS):
                    dve.wait_ge(y_psum, b * EXPERTS + (e + 1))
                    dve.wait_ge(y_used, b * EXPERTS + e)
                    for q in range(TPB):
                        ins = V.scalar_tensor_tensor(out=acc[:, bass.ts(b * TPB + q, 1), :].rearrange("p a d -> p (a d)"),
                                                     in0=ps[:, 4 + e % 2, P * q:P * (q + 1)],
                                                     scalar=coef[:, bass.ts(b * TPB + q, 1), e:e + 1].rearrange("p a d -> p (a d)"),
                                                     in1=acc[:, bass.ts(b * TPB + q, 1), :].rearrange("p a d -> p (a d)"),
                                                     op0=ALU.mult, op1=ALU.add)
                    ins.then_inc(y_used, 1)
            dve.wait_ge(y_used, BATCH * EXPERTS)
            V.tensor_tensor(att[:], att[:], amem[:], ALU.add).then_inc(acc_ready, 1)
            dve.wait_ge(acc_ready, 1)
            for b in range(BATCH):
                r = slice(b * TPB, (b + 1) * TPB)
                dve.wait_ge(silu_ready, b + 1)
                V.tensor_tensor(att[:, r, :], att[:, r, :], acc[:, r, :], ALU.mult).then_inc(fchain, 1)
                dve.wait_ge(fchain, b + 1)
                V.tensor_tensor(xs[:, r, :], xs[:, r, :], att[:, r, :], ALU.add).then_inc(fin_ready, 1)

        @block.tensor
        def _(pe):
            T = nc.tensor

            def turn(st, b):
                pe.wait_ge(xn_ready, b + 1)
                if st >= 2:
                    pe.wait_ge(xnT_ready, b - 1)
                for q in range(TPB):
                    ins = T.transpose(ps[:, st % 2, P * q:P * (q + 1)], xn[:, b * TPB + q, :], ident[:])
                ins.then_inc(xT_psum, 1)

            def project(st, b):
                pe.wait_ge(xT_ready, b + 1)
                if st >= 1:
                    pe.wait_ge(q_neg_ready, 2 * b)
                T.matmul(ps[:, 3, :], wqp[:], xT[:, st % 2, :], start=True, stop=True).then_inc(q_psum, 1)
                if st >= 1:
                    pe.wait_ge(vr_used, 2 * b)
                for q in range(TPB):
                    ins = T.matmul(ps[:, 2, 80 * q:80 * q + 80], xT[:, st % 2, P * q:P * (q + 1)], wvr[:],
                                   start=True, stop=True)
                ins.then_inc(vr_psum, 1)

            def memory(st, b):
                pe.wait_ge(sigma_ready, b + 1)
                if st >= 1:
                    pe.wait_ge(mem_used, b)
                for q in range(TPB):
                    ins = T.matmul(ps[:, 4 + q // 2, 256 * (q % 2):256 * (q % 2) + 2 * MEMW], sigma[:, P * q:P * (q + 1)],
                                   memb[:], start=True, stop=True)
                ins.then_inc(mem_psum, 1)

            pe.wait_ge(in_w, 160)

            turn(0, 0)
            for b in range(BATCH):
                project(b, b)
                if b + 1 < BATCH:
                    turn(b + 1, b + 1)
                memory(b, b)

            def keys(st, b):
                T.matmul(ps[:, 7, :], wks[:, st % 4, :], xnT[:, bass.ts(b, SEQ)], start=True, stop=True).then_inc(ka_psum, 1)

            def queries(st, b):
                T.matmul(ps[:, 7, :], wqs[:, st % 4, :], xnT[:, bass.ts(b, SEQ)], start=True, stop=True).then_inc(qa_psum, 1)

            def pv(st, u, c):
                if c == 0:
                    pe.wait_ge(v_ready, u + 1)
                    if st >= 1:
                        pe.wait_ge(pv_copied, u)
                pe.wait_ge(p_ready, u * 16 + (4 * c + 4))
                for j in range(4):
                    v0 = VW * (j // 2)
                    ins = T.matmul(ps[32 * j:32 * j + 32, 6, :], v_unit[:, st % 4, c, v0:v0 + 32],
                                   probs[:, 4 * (c % 2) + j, :], start=(c == 0), stop=(c == 3))
                ins.then_inc(pv_psum, 1)

            def step(st, t, batch, half):
                a_on, b_on, m_on, c_on, o_on = (in_range(st + d) for d in (1, 0, -1, -2, -3))
                if c_on:
                    pe.wait_ge(m_rows, (t - 1) * 32)
                if m_on:
                    pe.wait_ge(max_ready, t * 8)
                    if in_range(st - 4):
                        pe.wait_ge(att_ready, t - 3)
                    elif in_range(st):
                        pe.wait_ge(qs_ready, t + 1)
                    T.transpose(ps[0:16, 7, 0:P], neg_max[:, (st - 1) % 2, :], ident[:]).then_inc(mt_psum, 1)
                for c in range(4):
                    if c_on:
                        for j in range(4):
                            n = 4 * c + j
                            if st - 2 >= 1 or n >= 2:
                                pe.wait_ge(p_ready, (t - 2) * 16 + (n - 1))
                            T.matmul(ps[:, 4 + n % 2, :], k_zero[:, (st - 2) % 4, j, P * c:P * (c + 1)],
                                     q_stack[:, (st - 2) % 4, :], start=True, stop=True).then_inc(st_psum, 1)
                    if c == 0 and a_on:
                        if m_on:
                            pe.wait_ge(m_ready, t)
                        else:
                            pe.wait_ge(qs_ready, 1)
                        keys(st + 1, batch(1))
                    if c == 1 and a_on:
                        pe.wait_ge(ks_ready, t + 2)
                        queries(st + 1, batch(1))
                    if b_on:
                        if c == 0:
                            pe.wait_ge(kz_ready[st % 2], half(2) * 64)
                            pe.wait_ge(qs_ready, t + 1)
                        for j in range(4):
                            if j % 2 == 0 and (st >= 1 or c >= 1):
                                pe.wait_ge(max_ready, t * 8 + (2 * c + j // 2 - 1))
                            ins = T.matmul(ps[:, j, :], q_stack[:, st % 4, P * c:P * (c + 1)],
                                           k_zero[:, st % 4, j, :], start=True, stop=True)
                            if j % 2:
                                ins.then_inc(s_psum, 1)
                    if c == 0 and o_on:
                        pv(st - 3, t - 3, 3)
                    if c >= 1 and c_on:
                        pv(st - 2, t - 2, c - 1)
                    if c == 2 and o_on:
                        pe.wait_ge(pv_copied, t - 2)
                        if a_on:
                            pe.wait_ge(qs_ready, t + 2)
                        elif m_on:
                            pe.wait_ge(m_ready, t)
                        else:
                            pe.wait_ge(att_ready, t - 3)
                        for q in range(TPB):
                            ins = T.transpose(ps[:, 7, P * q:P * (q + 1)], pv_sb[:, P * q:P * (q + 1)], ident[:])
                        ins.then_inc(o_psum, 1)

            pe.wait_ge(xnT_ready, BATCH)
            keys(0, 0)
            pe.wait_ge(ks_ready, 1)
            queries(0, 0)
            pe.wait_ge(mem_used, BATCH)
            unit_loop(pe, step)

            pe.wait_ge(in_ffn, 64)
            def up(b, e):
                for f in range(FT):
                    T.matmul(ps[:, f, :], w1s[:, e, P * f:P * (f + 1)], xnT[:, bass.ts(b, SEQ)],
                             start=True, stop=True).then_inc(h_psum, 1)
            with pe.Fori(0, BATCH) as b:
                for e in range(EXPERTS):
                    pe.wait_ge(h_ready, b * (EXPERTS * FT) + e * FT)
                    up(b, e)
                    if e >= 2:
                        pe.wait_ge(y_used, b * EXPERTS + (e - 1))
                    else:
                        pe.wait_ge(y_used, b * EXPERTS)
                    pe.wait_ge(h_ready, b * (EXPERTS * FT) + (e + 1) * FT)
                    for q in range(TPB):
                        o = ps[:, 4 + e % 2, P * q:P * (q + 1)]
                        T.matmul(o, one_row[:], b2s[:, e, :], start=True, stop=False)
                        for f in range(FT):
                            ins = T.matmul(o, hidden[:, 4 * (e % 2) + f, P * q:P * (q + 1)], w2s[:, e, f, :],
                                           start=False, stop=(f == FT - 1))
                    ins.then_inc(y_psum, 1)


def kernel(**inputs):
    import concourse.bacc as bacc
    from concourse.bass_utils import run_bass_kernel_spmd

    a = {k[3:]: np.ascontiguousarray(v) for k, v in inputs.items()}
    f32 = a["attn_x"].dtype
    wq_stack = np.zeros((DM, GROUPS, 4, 4, DH), f32)
    wk_stack = np.zeros((DM, GROUPS, 4, 4, DH), f32)
    for h in range(HEADS):
        for part in range(3):
            kv = h // (HEADS // KVH)
            wq_stack[:, h // 4, h % 4, part] = a["attn_Wq"][:, h * DH:(h + 1) * DH]
            wk_stack[:, h // 4, h % 4, part] = a["attn_Wk"][:, kv * DH:(kv + 1) * DH]
    wv_router = np.zeros((DM, VCOLS + EXPERTS), f32)
    for kv in range(KVH):
        wv_router[:, kv * VW:kv * VW + DH] = a["attn_Wv"][:, kv * DH:(kv + 1) * DH]
    wv_router[:, VCOLS:] = a["ffn_router_w"].T
    mem_block = np.zeros((DM, 2 * MEMW), f32)
    for g in range(2):
        mem_block[64 * g:64 * g + 64, MEMW * g:MEMW * g + 64] = a["attn_memory"]
        mem_block[64 * g:64 * g + 64, MEMW * g + 64] = a["attn_memory_norm"]
    row = np.arange(P) % 32
    signs = np.zeros((P, 2), f32)
    signs[(row >= 16) & (row < 24), 0] = -1.0
    signs[(row >= 8) & (row < 16), 1] = -1.0
    signs[(row == 24) | (row == 25), 1] = 1.0
    ones = np.zeros((P, 1), f32)
    ones[(row == 24) | (row == 25), 0] = 1.0
    arrays = {
        "x": a["attn_x"],
        "wq_stack": wq_stack.reshape(DM, GROUPS, P),
        "wk_stack": wk_stack.reshape(DM, GROUPS, P),
        "wq": a["attn_Wq"],
        "wv_router": wv_router,
        "mem_block": mem_block,
        "mem_weight": a["attn_memory_weight"],
        "w1": np.ascontiguousarray(a["ffn_w1"].transpose(2, 0, 1)),
        "b1": np.ascontiguousarray(a["ffn_b1"].reshape(EXPERTS, FT, P).transpose(2, 0, 1)),
        "w2": np.ascontiguousarray(a["ffn_w2"].reshape(EXPERTS, DM, FT, P).transpose(3, 0, 2, 1)),
        "b2": a["ffn_b2"].reshape(1, EXPERTS, DM),
        "ident": np.eye(P, dtype=f32),
        "signs": signs,
        "ones": ones,
        "iota": np.tile(np.arange(EXPERTS, dtype=f32), (P, 1)),
    }
    nc = bacc.Bacc("TRN2", target_bir_lowering=False, num_devices=1)
    args = [nc.dram_tensor(f"in_{k}", v.shape, mybir.dt.from_np(v.dtype), kind="ExternalInput").ap()
            for k, v in arrays.items()]
    out = nc.dram_tensor("out", arrays["x"].shape, F32, kind="ExternalOutput").ap()
    build(nc, *args, out)
    r = run_bass_kernel_spmd(nc, [{f"in_{k}": v for k, v in arrays.items()}], core_ids=[0])
    return r.results[0]["out"]
```

```python
from contextlib import ExitStack

import numpy as np

import concourse.bass as bass
from concourse import mybir

F32 = mybir.dt.float32
F32R = mybir.dt.float32r
U32 = mybir.dt.uint32
I32 = mybir.dt.int32
ALU = mybir.AluOpType
ACT = mybir.ActivationFunctionType
AX = mybir.AxisListType

P = 128
BATCH, SEQ, DM = 8, 512, 128
HEADS, DH, KVH = 16, 8, 8
TILES = BATCH * SEQ // P
TPB = SEQ // P
GROUPS = 4
UNITS = BATCH * GROUPS
EXPERTS, FF, TOP = 8, 512, 2
FT = FF // P
BS = 512
BLOCKS = (TOP * BATCH * SEQ + EXPERTS * (BS - 1)) // BS
XW = DM + 1
VW = DH + 1
VCOLS = KVH * VW
VR = VCOLS + EXPERTS
MEMW = 65
LN_EPS = 1e-5
SCALE = 1.0 / float(np.sqrt(DH))
STEPS = UNITS + 3
FIRST_BLOCK = 4

C_IDENT, C_BELOW, C_ONES = 0, P, 2 * P
C_IOTA, C_FILL, C_BLOCK = 3 * P, 3 * P + 8, 3 * P + 16
C_NEXT = C_BLOCK + BLOCKS
C_QSIGN = C_NEXT + EXPERTS * TILES
C_KSIGN, C_KONE = C_QSIGN + 1, C_QSIGN + 2
C_ALL = C_QSIGN + 3


def front_loop(eng, step, extra):
    step(0, 0)
    with eng.Fori(0, 3) as i:
        for s in (1, 2):
            step(s, i * 2 + s)
    for b in range(7, BATCH + extra):
        step(b, b)


def unit_loop(eng, step):
    first, last = 8, 24
    for t in range(first):
        step(t, t, lambda k: (t + k) // 4, lambda k: (t + k) // 2)
    with eng.Fori(0, (last - first) // 4) as i:
        for s in range(first, first + 4):
            step(s, i * 4 + s, lambda k: i + (s + k) // 4, lambda k: i * 2 + (s + k) // 2)
    for t in range(last, STEPS):
        step(t, t, lambda k: (t + k) // 4, lambda k: (t + k) // 2)


def has_unit(u):
    return 0 <= u < UNITS


def has_block(n):
    return 0 <= n < BLOCKS


def build(nc, x, wq_stack, wk_stack, wq, wv_router, mem_block, mem_weight, w_experts, b_experts, consts_in, out):
    ctx = ExitStack()
    with ctx:
        def sb(name, shape, dt=F32):
            return ctx.enter_context(nc.sbuf_tensor(name, shape, dt))

        def sem(name):
            return ctx.enter_context(nc.semaphore(name))

        x_slots = nc.dram_tensor("x_slots", [BLOCKS * BS, XW], F32, kind="Internal").ap()
        y_slots = nc.dram_tensor("y_slots", [BLOCKS * BS, DM], F32, kind="Internal").ap()

        consts = sb("consts", [P, C_ALL])
        ident = consts[:, C_IDENT:C_IDENT + P]
        below = consts[:, C_BELOW:C_BELOW + P]
        ones = consts[:, C_ONES:C_ONES + P]
        iota = consts[:, C_IOTA:C_IOTA + EXPERTS]
        fills = consts[:, C_FILL:C_FILL + 8]
        block_no = consts[:, C_BLOCK:C_BLOCK + BLOCKS]
        carry = consts[:, C_NEXT:C_NEXT + EXPERTS * TILES]
        q_sign, k_sign, k_one = (consts[:, c:c + 1] for c in (C_QSIGN, C_KSIGN, C_KONE))
        xs = sb("xs", [P, TILES, DM])
        xn = sb("xn", [P, TILES, XW])
        xnT = sb("xnT", [P, BATCH * SEQ])
        att = sb("att", [P, TILES, DM])
        values = sb("values", [P, TILES, VCOLS])
        logits = sb("logits", [P, TILES, EXPERTS])
        wqs = sb("wqs", [P, GROUPS, P])
        wks = sb("wks", [P, GROUPS, P])
        wqp = sb("wqp", [P, DM])
        wvr = sb("wvr", [P, VR])
        memb = sb("memb", [P, 2 * MEMW])
        mw = sb("mw", [P, 1])
        tanh_w = sb("tanh_w", [P, 1])
        w_mem = sb("w_mem", [P, 1])
        w_dot = sb("w_dot", [P, 1])
        eps = sb("eps", [P, 1])
        stats = sb("stats", [P, TILES, 6])
        mv = sb("mv", [P, TILES, 2])
        std = sb("std", [P, TILES])
        rstd = sb("rstd", [P, TILES])
        mden = sb("mden", [P, TPB, 2])
        mden_w = sb("mden_w", [P, TPB, 2])
        q_hi = sb("q_hi", [P, SEQ], F32R)
        k_hi = sb("k_hi", [P, SEQ], F32R)
        q_stack = sb("q_stack", [P, 4, SEQ], F32R)
        k_stack = sb("k_stack", [P, 2, SEQ], F32R)
        k_zero = sb("k_zero", [P, 4, 4, SEQ], F32R)
        v_unit = sb("v_unit", [P, 4, TPB, 2 * VW + 23])
        neg_max = sb("neg_max", [P, 2, 16])
        m_hi = sb("m_hi", [16, P], F32R)
        m_lo = sb("m_lo", [16, P], F32R)
        probs = sb("probs", [P, 8, SEQ])
        pv_sb = sb("pv_sb", [P, SEQ])
        rden = sb("rden", [P, TPB, 4])
        o_tmp = sb("o_tmp", [P, TPB, 4 * DH])
        scratch = sb("scratch", [P, 4200])
        w_raw = scratch[:, 0:1024]
        x_rows = scratch[:, 1024:1024 + 2 * 4 * XW].rearrange("p (b q d) -> p b q d", b=2, q=4)
        h_f32 = scratch[:, 2064:2064 + 1024].rearrange("p (b s) -> p b s", b=2)
        y_sb = scratch[:, 3088:3088 + BS]
        y_rows = scratch[:, 3600:3600 + BS].rearrange("p (q d) -> p q d", q=4)
        bias = sb("bias", [P, 2, FT + 1])
        w_hi = sb("w_hi", [P, 2 * FF], F32R)
        w_lo = sb("w_lo", [P, 2 * FF], F32R)
        x_hi = sb("x_hi", [P, BS], F32R)
        x_lo = sb("x_lo", [P, BS], F32R)
        h_hi = sb("h_hi", [P, FT, BS], F32R)
        h_lo = sb("h_lo", [P, FT, BS], F32R)
        xT = scratch[:, 0:1024].rearrange("p (b s) -> p b s", b=2)
        q_neg, q_pos, q_exp, q_tanh, sigma = (scratch[:, 1024 + 512 * k:1536 + 512 * k] for k in range(5))
        chosen0, chosen1, chosen, upto, slot_all, prod = (
            probs[:, k // 2, 256 * (k % 2):256 * (k % 2) + 256].rearrange("p (e t) -> p e t", e=EXPERTS) for k in range(6))
        top = probs[:, 3, 0:256].rearrange("p (t e) -> p t e", e=8)
        over = probs[:, 3, 256:320].rearrange("p (e j) -> p e j", e=EXPERTS)
        passed = probs[:, 4, 0:BLOCKS * EXPERTS].rearrange("p (n e) -> p n e", e=EXPERTS)
        top_f = sb("top_f", [P, TILES, 2])
        top_i = sb("top_i", [P, TILES, 8], U32)
        gap = sb("gap", [P, TILES])
        tgap = sb("tgap", [P, TILES])
        gates = sb("gates", [P, 2, TILES])
        small = sb("small", [P, 6, 8])
        row_sum, blocks_of, end_block, start_block, base = (small[:, k, :] for k in range(5))
        slot_f = sb("slot_f", [P, 2, TILES])
        slots = sb("slots", [P, 2, TILES], U32)
        expert_f = sb("expert_f", [P, BLOCKS])
        expert_of = sb("expert_of", [P, BLOCKS], I32)

        ps = ctx.enter_context(nc.psum_tensor("ps", [P, 8, SEQ], F32))

        in_w = sem("in_w")
        in_x = [sem(f"in_x{b}") for b in range(BATCH)]
        setup = sem("setup")
        zero_slots = sem("zero_slots")
        chain, q_chain, m_chain, r_chain, o_chain, f_chain = (
            sem(k) for k in ("chain", "q_chain", "m_chain", "r_chain", "o_chain", "f_chain"))
        var_ready, std_ready, xn_ready, mw_ready = (sem(k) for k in ("var_ready", "std_ready", "xn_ready", "mw_ready"))
        xT_psum, xT_ready, xnT_ready = sem("xT_psum"), sem("xT_ready"), sem("xnT_ready")
        vr_psum, vr_used = sem("vr_psum"), sem("vr_used")
        gap_ready, tgap_ready, sums_ready, sums_psum = (
            sem(k) for k in ("gap_ready", "tgap_ready", "sums_ready", "sums_psum"))
        gate_ready, slots_ready, experts_ready = sem("gate_ready"), sem("slots_ready"), sem("experts_ready")
        scattered = [sem("scattered0"), sem("scattered1")]
        q_psum, q_neg_ready, q_act_ready, sigma_ready = (
            sem(k) for k in ("q_psum", "q_neg_ready", "q_act_ready", "sigma_ready"))
        mem_psum, mem_used = sem("mem_psum"), sem("mem_used")
        ka_psum, k_hi_ready, ks_ready = sem("ka_psum"), sem("k_hi_ready"), sem("ks_ready")
        kz_ready = [sem("kz_ready0"), sem("kz_ready1")]
        qa_psum, q_hi_ready, qs_ready = sem("qa_psum"), sem("q_hi_ready"), sem("qs_ready")
        s_psum, max_ready = sem("s_psum"), sem("max_ready")
        mt_psum, m_hi_ready, m_ready, m_rows = sem("mt_psum"), sem("m_hi_ready"), sem("m_ready"), sem("m_rows")
        st_psum, p_ready = sem("st_psum"), sem("p_ready")
        v_ready = sem("v_ready")
        pv_psum, pv_copied = sem("pv_psum"), sem("pv_copied")
        o_psum, att_ready = sem("o_psum"), sem("att_ready")
        block_in = [sem("block_in0"), sem("block_in1")]
        w_hi_ready, w_split = sem("w_hi_ready"), sem("w_split")
        xt_psum, x_hi_ready, x_lo_ready = sem("xt_psum"), sem("x_hi_ready"), sem("x_lo_ready")
        h_psum, h_ready, h_hi_ready, h_lo_ready = (sem(k) for k in ("h_psum", "h_ready", "h_hi_ready", "h_lo_ready"))
        y_psum, y_copied, yt_psum, yt_ready, y_stored = (
            sem(k) for k in ("y_psum", "y_copied", "yt_psum", "yt_ready", "y_stored"))
        gathered = [sem("gathered0"), sem("gathered1")]
        x_again, silu_ready, fin_ready, stored = (sem(k) for k in ("x_again", "silu_ready", "fin_ready", "stored"))

        block = ctx.enter_context(nc.Block())

        x_view = x.rearrange("b (q p) d -> p b q d", p=P)
        out_view = out.rearrange("b (q p) d -> p b q d", p=P)
        x_slot_blocks = x_slots.rearrange("(n p q) d -> n p (q d)", p=P, q=4)
        y_slot_blocks = y_slots.rearrange("(n p q) d -> n p (q d)", p=P, q=4)
        W_LOADS = 7

        @block.sync
        def _(sp):
            sp.dma_start(consts[:], consts_in).then_inc(in_w, 16)
            for b in range(BATCH):
                sp.dma_start(xs[:, b * TPB:(b + 1) * TPB, :], x_view[:, b]).then_inc(in_x[b], 16)
                if b == 1:
                    for dst, src in ((wvr[:], wv_router), (mw[:], mem_weight.partition_broadcast(P)), (wqp[:], wq),
                                     (memb[:], mem_block), (wqs[:], wq_stack), (wks[:], wk_stack)):
                        sp.dma_start(dst, src).then_inc(in_w, 16)
            sp.wait_ge(setup, 1)
            for n in range(BLOCKS):
                sp.dma_start(x_slot_blocks[n], k_zero[:, 3].bitcast(F32).rearrange("p j s -> p (j s)")[:, 0:4 * XW])\
                  .then_inc(zero_slots, 16)

            def place_keys(st):
                for j in range(4):
                    r = slice(32 * j, 32 * j + 32)
                    sp.dma_start(k_zero[r, st % 4, j, :].bitcast(F32),
                                 k_stack[r, st % 2, :].bitcast(F32)).then_inc(kz_ready[st % 2], 16)

            def load_block(st, n):
                e = sp.value_load(expert_of[0:1, n:n + 1] if isinstance(n, int) else expert_of[0:1, bass.ds(n, 1)],
                                  min_val=0, max_val=EXPERTS - 1)
                sp.dma_start(w_raw, w_experts[bass.ds(e, 1)].rearrange("a p w -> p (a w)")).then_inc(block_in[st % 2], 16)
                sp.dma_start(bias[:, st % 2, :],
                             b_experts[bass.ds(e, 1)].rearrange("a p w -> p (a w)")).then_inc(block_in[st % 2], 16)
                sp.dma_start(x_rows[:, st % 2].rearrange("p q d -> p (q d)"),
                             x_slot_blocks[n] if isinstance(n, int) else
                             x_slot_blocks[bass.ds(n, 1)].rearrange("a p w -> p (a w)")).then_inc(block_in[st % 2], 16)

            def step(st, t, batch, half):
                if has_unit(st + 1):
                    sp.wait_ge(ks_ready, t + 2)
                    place_keys(st + 1)
                if has_unit(st - 1):
                    sp.wait_ge(m_ready, t)
                    for row, part in ((24, m_hi), (25, m_lo)):
                        sp.dma_start(q_stack[row:P:32, (st - 1) % 4, :].bitcast(F32),
                                     part[:].bitcast(F32)).then_inc(m_rows, 16)
                if has_block(st - 5):
                    sp.wait_ge(yt_ready, t - 4)
                    sp.dma_start(y_slot_blocks[t - 5] if isinstance(t, int) else
                                 y_slot_blocks[bass.ds(t - 5, 1)].rearrange("a p w -> p (a w)"),
                                 y_rows.rearrange("p q d -> p (q d)")).then_inc(y_stored, 16)
                if has_block(st - 3):
                    if st == 3:
                        sp.wait_ge(experts_ready, 1)
                        for k in range(2):
                            sp.wait_ge(scattered[k], 16 * TILES)
                        sp.wait_ge(mem_used, BATCH)
                    else:
                        sp.wait_ge(w_split, t - 3)
                    load_block(st - 3, t - 3)

            sp.wait_ge(zero_slots, 16 * BLOCKS)
            sp.wait_ge(ks_ready, 1)
            place_keys(0)
            unit_loop(sp, step)

            sp.wait_ge(qa_psum, UNITS)
            sp.dma_start(xnT[:].rearrange("p (b q d) -> p b q d", b=BATCH, q=TPB), x_view).then_inc(x_again, 16)
            for b in range(BATCH):
                sp.wait_ge(fin_ready, b + 1)
                sp.dma_start(out_view[:, b], att[:, b * TPB:(b + 1) * TPB, :]).then_inc(stored, 16)
            sp.wait_ge(stored, 16 * BATCH)

        @block.gpsimd
        def _(pool):
            pool.memset(k_zero[:].bitcast(F32), 0.0).then_inc(setup, 1)
            pool.memset(values[:], 1.0).then_inc(setup, 1)
            pool.memset(v_unit[:], 0.0).then_inc(setup, 1)
            pool.wait_ge(setup, 3)
            pool.wait_ge(vr_used, 2 * BATCH)

            def unit_values(g, b):
                pool.tensor_copy(v_unit[:, g, :, 0:2 * VW],
                                 values[:, bass.ts(b, TPB), 2 * VW * g:2 * VW * (g + 1)]).then_inc(v_ready, 1)

            for g in range(4):
                unit_values(g, 0)
            pool.wait_ge(zero_slots, 16 * BLOCKS)
            for k in range(2):
                pool.wait_ge(slots_ready, 1)
                pool.wait_ge(gate_ready, k + 1)
                for t in range(TILES):
                    pool.indirect_dma_start(out=x_slots, out_offset=bass.IndirectOffsetOnAxis(ap=slots[:, k, t:t + 1], axis=0),
                                            in_=xn[:, t, :], in_offset=None).then_inc(scattered[k], 16)

            def step(st, t, b, half_m2):
                if has_unit(st):
                    pool.wait_ge(pv_psum, (t - 3) * TPB)
                    unit_values(st % 4, b)
                if has_block(st - FIRST_BLOCK):
                    pool.wait_ge(block_in[st % 2], half_m2 * 48)
                    if st > FIRST_BLOCK:
                        pool.wait_ge(y_psum, t - 4)
                    pool.tensor_tensor(w_hi[:], w_raw, ones[:, 0:1].to_broadcast([P, 2 * FF]), ALU.mult).then_inc(w_hi_ready, 1)
                    pool.wait_ge(w_hi_ready, t - 3)
                    pool.tensor_tensor(w_lo[:], w_raw, w_hi[:].bitcast(F32), ALU.subtract).then_inc(w_split, 1)

            for t in range(4, 8):
                step(t, t, t // 4, (t - 2) // 2)
            with pool.Fori(0, 4) as i:
                for s in range(8, 12):
                    step(s, i * 4 + s, i + 2, i * 2 + (s - 2) // 2)
            for t in range(24, UNITS):
                step(t, t, t // 4, (t - 2) // 2)
            pool.wait_ge(y_stored, 16 * BLOCKS)
            for k in range(2):
                if k:
                    pool.wait_ge(gathered[0], 16 * TILES)
                for t in range(TILES):
                    pool.indirect_dma_start(out=xs[:, t, :], out_offset=None, in_=y_slots,
                                            in_offset=bass.IndirectOffsetOnAxis(ap=slots[:, k, t:t + 1], axis=0),
                                            compute_op=ALU.add if k else ALU.bypass).then_inc(gathered[k], 16)

        @block.scalar
        def _(act):
            A = nc.scalar
            act.wait_ge(var_ready, 1)
            A.activation(std[:], mv[:, :, 1], ACT.Sqrt, bias=eps[:]).then_inc(std_ready, 1)
            act.wait_ge(in_w, 16 * W_LOADS)
            A.activation(tanh_w[:], mw[:], ACT.Tanh, scale=0.5).then_inc(mw_ready, 1)

            def features(st, b):
                act.wait_ge(xT_psum, b + 1)
                if st >= 2:
                    act.wait_ge(vr_psum, b - 1)
                A.copy(xT[:, st % 2, :], ps[:, st % 2, :]).then_inc(xT_ready, 1)
            front_loop(act, features, 0)

            act.wait_ge(gap_ready, 1)
            A.activation(tgap[:], gap[:], ACT.Tanh, scale=0.5).then_inc(tgap_ready, 1)

            def elu(st, b):
                act.wait_ge(q_psum, b + 1)
                if st >= 1:
                    act.wait_ge(sigma_ready, b)
                A.activation(q_pos, ps[:, 5 + st % 2, :], ACT.Relu).then_inc(q_act_ready, 1)
                act.wait_ge(q_neg_ready, b + 1)
                A.activation(q_exp, q_neg, ACT.Exp).then_inc(q_act_ready, 1)
                A.activation(q_tanh, q_neg, ACT.Tanh, scale=0.5).then_inc(q_act_ready, 1)
            front_loop(act, elu, 0)

            def exps(st, u, c, js):
                for j in js:
                    n = 4 * c + j
                    act.wait_ge(st_psum, u * 16 + (n + 1))
                    if j == 0 and (st >= 1 or c >= 2):
                        act.wait_ge(pv_psum, u * 4 + (c - 1))
                    A.activation(probs[:, n % 8, :], ps[:, 4 + n % 2, :], ACT.Exp, scale=SCALE).then_inc(p_ready, 1)

            def keys_hi(u):
                act.wait_ge(ka_psum, u + 1)
                A.activation(k_hi[:], ps[:, 7, :], ACT.Identity, bias=k_one).then_inc(k_hi_ready, 1)

            def queries_hi(u):
                act.wait_ge(qa_psum, u + 1)
                A.copy(q_hi[:], ps[:, 7, :]).then_inc(q_hi_ready, 1)

            def step(st, t, batch, half):
                c_on, o_on = has_unit(st - 2), has_unit(st - 3)
                for c in range(4):
                    if c_on:
                        exps(st - 2, t - 2, c, (0,))
                    if c == 0 and has_block(st - 5):
                        act.wait_ge(y_psum, t - 4)
                        if st - 5 >= 1:
                            act.wait_ge(yt_psum, t - 5)
                        A.activation(y_sb, ps[:, 2, :], ACT.Identity, bias=bias[:, (st - 5) % 2, FT:FT + 1])\
                         .then_inc(y_copied, 1)
                    if c == 1 and o_on:
                        act.wait_ge(pv_psum, (t - 2) * 4)
                        if st - 3 >= 1:
                            act.wait_ge(o_psum, t - 3)
                        A.copy(pv_sb[:], ps[:, 6, :]).then_inc(pv_copied, 1)
                    if c_on:
                        exps(st - 2, t - 2, c, (1, 2))
                    if c == 0 and has_unit(st + 1):
                        act.wait_ge(ks_ready, t + 1)
                        keys_hi(t + 1)
                    if c == 2 and has_unit(st + 1):
                        act.wait_ge(qs_ready, t + 1)
                        queries_hi(t + 1)
                    if c_on:
                        exps(st - 2, t - 2, c, (3,))
                    if c == 2 and has_block(st - 4):
                        act.wait_ge(xt_psum, t - 3)
                        if st > FIRST_BLOCK:
                            act.wait_ge(y_psum, t - 4)
                        A.copy(x_hi[:], ps[:, 2, :]).then_inc(x_hi_ready, 1)
                if has_block(st - 4):
                    for f in range(FT):
                        act.wait_ge(h_psum, t * 4 + (f - 15))
                        if st > FIRST_BLOCK or f >= 2:
                            act.wait_ge(h_lo_ready, t * 4 + (f - 17))
                        A.activation(h_f32[:, f % 2, :], ps[:, 2 + f % 2, :], ACT.Gelu,
                                     bias=bias[:, (st - 4) % 2, f:f + 1]).then_inc(h_ready, 1)

            keys_hi(0)
            queries_hi(0)
            unit_loop(act, step)

            act.wait_ge(gathered[0], 16 * TILES)
            act.wait_ge(gathered[1], 16 * TILES)
            for b in range(BATCH):
                r = slice(b * TPB, (b + 1) * TPB)
                A.activation(xs[:, r, :], xs[:, r, :], ACT.Silu).then_inc(silu_ready, 1)

        @block.vector
        def _(dve):
            V = nc.vector
            V.memset(eps[:], LN_EPS)
            for b in range(BATCH):
                dve.wait_ge(in_x[b], 16)
                for t in range(b * TPB, (b + 1) * TPB):
                    V.bn_stats(stats[:, t, :], xs[:, t, :]).then_inc(chain, 1)
            dve.wait_ge(chain, TILES)
            for t in range(TILES):
                ins = V.bn_aggr(mv[:, t, :], stats[:, t, :])
            ins.then_inc(var_ready, 1)
            dve.wait_ge(std_ready, 1)
            V.reciprocal(rstd[:], std[:]).then_inc(chain, 1)
            dve.wait_ge(chain, TILES + 1)
            for t in range(TILES):
                ins = V.tensor_scalar(xn[:, t, 0:DM], xs[:, t, :], mv[:, t, 0:1], rstd[:, t:t + 1],
                                      ALU.subtract, ALU.mult)
                if t % TPB == TPB - 1:
                    ins.then_inc(xn_ready, 1)
            dve.wait_ge(mw_ready, 1)
            V.tensor_scalar(w_mem[:], tanh_w[:], 0.5, 0.5, ALU.mult, ALU.add).then_inc(chain, 1)
            V.tensor_scalar(w_dot[:], tanh_w[:], -0.5, 0.5, ALU.mult, ALU.add).then_inc(chain, 1)
            dve.wait_ge(chain, TILES + 3)
            dve.wait_ge(setup, 3)

            def features(st, b):
                if st < BATCH:
                    dve.wait_ge(xT_psum, b + 1)
                    dve.wait_ge(xT_ready, b + 1)
                    V.tensor_copy(xnT[:, bass.ts(b, SEQ)], ps[:, st % 2, :]).then_inc(xnT_ready, 1)
                if st >= 1:
                    dve.wait_ge(vr_psum, b)
                    vr = ps[:, 2 + (st - 1) % 2, 0:TPB * VR].rearrange("p (t c) -> p t c", t=TPB)
                    V.tensor_scalar(values[:, bass.ts(b - 1, TPB), :].rearrange("p t (h c) -> p t h c", c=VW)[:, :, :, 0:DH],
                                    vr[:, :, 0:VCOLS].rearrange("p t (h c) -> p t h c", c=VW)[:, :, :, 0:DH],
                                    w_dot[:], None, ALU.mult).then_inc(vr_used, 1)
                    V.tensor_copy(logits[:, bass.ts(b - 1, TPB), :], vr[:, :, VCOLS:VR]).then_inc(vr_used, 1)
            front_loop(dve, features, 1)
            dve.wait_ge(vr_used, 2 * BATCH)

            count = [0]

            def link(ins, wait=True):
                count[0] += 1
                ins.then_inc(r_chain, 1)
                if wait:
                    dve.wait_ge(r_chain, count[0])

            def wide(ap, axis):
                return ap.unsqueeze(axis).to_broadcast([P, EXPERTS, TILES])

            for t in range(TILES):
                link(V.max(top[:, t, :], logits[:, t, :]), wait=False)
            dve.wait_ge(r_chain, count[0])
            V.tensor_tensor(gap[:], top[:, :, 0], top[:, :, 1], ALU.subtract).then_inc(gap_ready, 1)
            for t in range(TILES):
                link(V.max_index(top_i[:, t, :], top[:, t, :], logits[:, t, :]), wait=False)
            dve.wait_ge(r_chain, count[0])
            link(V.tensor_copy(top_f[:], top_i[:, :, 0:2]))
            link(V.tensor_tensor(chosen0, wide(iota, 2), wide(top_f[:, :, 0], 1), ALU.is_equal), wait=False)
            link(V.tensor_tensor(chosen1, wide(iota, 2), wide(top_f[:, :, 1], 1), ALU.is_equal))
            link(V.tensor_tensor(chosen, chosen0, chosen1, ALU.add))
            flat = "p e t -> p (e t)"
            link(V.tensor_tensor_scan(upto.rearrange(flat), carry, chosen.rearrange(flat), 0.0, ALU.mult, ALU.add))
            V.tensor_copy(row_sum, upto[:, :, TILES - 1]).then_inc(sums_ready, 1)
            dve.wait_ge(tgap_ready, 1)
            link(V.tensor_scalar(gates[:, 0, :], tgap[:], 0.5, 0.5, ALU.mult, ALU.add), wait=False)
            link(V.tensor_scalar(gates[:, 1, :], tgap[:], -0.5, 0.5, ALU.mult, ALU.add))
            V.tensor_copy(xn[:, :, DM], gates[:, 0, :]).then_inc(gate_ready, 1)
            dve.wait_ge(sums_psum, 1)
            below_sum, all_sum = ps[:, 4, 0:8], ps[:, 4, 8:16]
            grid = [P, EXPERTS, 8]
            link(V.tensor_tensor(over, all_sum.unsqueeze(2).to_broadcast(grid), fills.unsqueeze(1).to_broadcast(grid), ALU.is_gt))
            link(V.tensor_reduce(blocks_of, over, AX.X, ALU.add))
            link(V.tensor_tensor_scan(end_block, ones[:, 0:8], blocks_of, 0.0, ALU.mult, ALU.add))
            link(V.tensor_tensor(start_block, end_block, blocks_of, ALU.subtract), wait=False)
            grid = [P, BLOCKS, EXPERTS]
            link(V.tensor_tensor(passed, end_block.unsqueeze(1).to_broadcast(grid), block_no.unsqueeze(2).to_broadcast(grid),
                                 ALU.is_le))
            link(V.scalar_tensor_tensor(out=base, in0=start_block, scalar=float(BS), in1=below_sum,
                                        op0=ALU.mult, op1=ALU.add), wait=False)
            link(V.tensor_reduce(expert_f[:], passed, AX.X, ALU.add), wait=False)
            link(V.tensor_tensor(slot_all, upto, chosen, ALU.subtract))
            link(V.tensor_tensor(slot_all, slot_all, wide(base, 2), ALU.add), wait=False)
            V.tensor_scalar(expert_of[:], expert_f[:], float(EXPERTS - 1), None, ALU.min).then_inc(experts_ready, 1)
            dve.wait_ge(r_chain, count[0])
            for k, pick in ((0, chosen0), (1, chosen1)):
                link(V.tensor_tensor(prod, pick, slot_all, ALU.mult))
                link(V.tensor_reduce(slot_f[:, k, :], prod.rearrange("p e t -> p t e"), AX.X, ALU.add))
            V.tensor_copy(slots[:], slot_f[:]).then_inc(slots_ready, 1)

            def memory(st, b):
                if st < BATCH:
                    dve.wait_ge(q_psum, b + 1)
                    dve.wait_ge(q_act_ready, b * 3 + 1)
                    V.tensor_scalar(q_neg, ps[:, 5 + st % 2, :], 0.0, None, ALU.min).then_inc(q_neg_ready, 1)
                if st >= 1:
                    dve.wait_ge(mem_psum, b)
                    k = (st - 1) % 2
                    num = ps[:, 2 * k:2 * k + 2, :].rearrange("p a (c n) -> p (a c) n", c=2)
                    V.reciprocal(mden[:], num[:, :, MEMW - 1:2 * MEMW:MEMW]).then_inc(m_chain, 1)
                    dve.wait_ge(m_chain, b * 2 - 1)
                    V.tensor_scalar(mden_w[:], mden[:], w_mem[:], None, ALU.mult).then_inc(m_chain, 1)
                    dve.wait_ge(m_chain, b * 2)
                    for g in range(2):
                        ins = V.tensor_tensor(att[:, bass.ts(b - 1, TPB), 64 * g:64 * g + 64],
                                              num[:, :, MEMW * g:MEMW * g + 64],
                                              mden_w[:, :, g:g + 1].to_broadcast([P, TPB, 64]), ALU.mult)
                    ins.then_inc(mem_used, 1)
                if st < BATCH:
                    dve.wait_ge(q_act_ready, b * 3 + 3)
                    V.scalar_tensor_tensor(out=q_exp, in0=q_exp, scalar=1.0, in1=q_tanh,
                                           op0=ALU.add, op1=ALU.mult).then_inc(q_chain, 1)
                    dve.wait_ge(q_chain, b + 1)
                    if st >= 1:
                        dve.wait_ge(mem_psum, b)
                    V.tensor_tensor(sigma, q_exp, q_pos, ALU.add).then_inc(sigma_ready, 1)
            front_loop(dve, memory, 1)
            dve.wait_ge(scattered[0], 16 * TILES)
            V.tensor_copy(xn[:, :, DM], gates[:, 1, :]).then_inc(gate_ready, 1)

            def stack(hi, sign, dst, ready):
                V.scalar_tensor_tensor(out=dst, in0=hi.bitcast(F32), scalar=sign, in1=ps[:, 7, :],
                                       op0=ALU.mult, op1=ALU.add).then_inc(ready, 1)

            def maxima(st, t, c, j):
                dve.wait_ge(s_psum, t * 16 + (4 * c + j + 1))
                if c == 0 and j == 0 and st >= 2:
                    dve.wait_ge(mt_psum, t - 1)
                V.tensor_reduce(neg_max[:, st % 2, 4 * j + c:4 * j + c + 1], ps[:, j % 2, :],
                                AX.X, ALU.max, negate=True).then_inc(max_ready, 1)

            def step(st, t, batch, half):
                for c in range(4):
                    if has_unit(st):
                        maxima(st, t, c, 0)
                        maxima(st, t, c, 1)
                    if c == 1 and has_block(st - 5):
                        dve.wait_ge(yt_psum, t - 4)
                        if st - 5 >= 1:
                            dve.wait_ge(y_stored, (t - 5) * 16)
                        V.tensor_tensor(y_rows, ps[:, 3, :].rearrange("p (q d) -> p q d", q=4),
                                        x_rows[:, (st - 5) % 2, :, DM:XW].to_broadcast([P, 4, DM]), ALU.mult)\
                         .then_inc(yt_ready, 1)
                    if c == 3 and has_block(st - 4):
                        dve.wait_ge(x_hi_ready, t - 3)
                        V.tensor_tensor(x_lo[:], ps[:, 2, :], x_hi[:].bitcast(F32), ALU.subtract).then_inc(x_lo_ready, 1)
                    if has_unit(st):
                        maxima(st, t, c, 2)
                    if c == 0 and has_unit(st + 1):
                        dve.wait_ge(k_hi_ready, t + 2)
                        if st + 1 >= 2:
                            dve.wait_ge(kz_ready[(st + 1) % 2], half(1) * 64)
                        if st + 1 >= 4:
                            dve.wait_ge(st_psum, (t - 2) * 16)
                        stack(k_hi[:], k_sign, k_stack[:, (st + 1) % 2, :], ks_ready)
                    if c == 1 and has_unit(st - 1):
                        dve.wait_ge(mt_psum, t)
                        if st - 1 >= 1:
                            dve.wait_ge(m_rows, (t - 1) * 32)
                        V.tensor_copy(m_hi[:], ps[0:16, 7, 0:P]).then_inc(m_hi_ready, 1)
                        dve.wait_ge(m_hi_ready, t)
                        V.tensor_tensor(m_lo[:], ps[0:16, 7, 0:P], m_hi[:].bitcast(F32), ALU.subtract).then_inc(m_ready, 1)
                    if c == 2 and has_unit(st + 1):
                        dve.wait_ge(q_hi_ready, t + 2)
                        stack(q_hi[:], q_sign, q_stack[:, (st + 1) % 4, :], qs_ready)
                    if c == 3 and has_unit(st - 3):
                        dve.wait_ge(o_psum, t - 2)
                        g, b = (st - 3) % 4, batch(-3)
                        o = ps[:, 7, :].rearrange("p (t j d) -> p t j d", t=TPB, j=4)
                        V.reciprocal(rden[:], o[:, :, :, DH]).then_inc(o_chain, 1)
                        dve.wait_ge(o_chain, t * 2 - 5)
                        V.tensor_tensor(o_tmp[:].rearrange("p t (j d) -> p t j d", j=4), o[:, :, :, 0:DH],
                                        rden[:].unsqueeze(3).to_broadcast([P, TPB, 4, DH]), ALU.mult).then_inc(o_chain, 1)
                        dve.wait_ge(o_chain, t * 2 - 4)
                        part = att[:, bass.ts(b, TPB), 32 * g:32 * g + 32]
                        V.tensor_tensor(part, part, o_tmp[:], ALU.add).then_inc(att_ready, 1)
                    if has_unit(st):
                        maxima(st, t, c, 3)
                if has_block(st - 4):
                    if st > FIRST_BLOCK:
                        dve.wait_ge(y_psum, t - 4)
                    for f in range(FT):
                        dve.wait_ge(h_ready, t * 4 + (f - 15))
                        V.tensor_copy(h_hi[:, f, :], h_f32[:, f % 2, :]).then_inc(h_hi_ready, 1)
                        dve.wait_ge(h_hi_ready, t * 4 + (f - 15))
                        V.tensor_tensor(h_lo[:, f, :], h_f32[:, f % 2, :], h_hi[:, f, :].bitcast(F32),
                                        ALU.subtract).then_inc(h_lo_ready, 1)
            dve.wait_ge(k_hi_ready, 1)
            stack(k_hi[:], k_sign, k_stack[:, 0, :], ks_ready)
            dve.wait_ge(q_hi_ready, 1)
            stack(q_hi[:], q_sign, q_stack[:, 0, :], qs_ready)
            unit_loop(dve, step)

            dve.wait_ge(x_again, 16)
            dve.wait_ge(att_ready, UNITS)
            for b in range(BATCH):
                r = slice(b * TPB, (b + 1) * TPB)
                dve.wait_ge(silu_ready, b + 1)
                V.tensor_tensor(att[:, r, :], att[:, r, :], xs[:, r, :], ALU.mult).then_inc(f_chain, 1)
                dve.wait_ge(f_chain, b + 1)
                V.tensor_tensor(att[:, r, :], att[:, r, :], xnT[:].rearrange("p (t d) -> p t d", d=DM)[:, r, :],
                                ALU.add).then_inc(fin_ready, 1)

        @block.tensor
        def _(pe):
            T = nc.tensor
            pe.wait_ge(in_w, 16 * W_LOADS)

            def turn(b):
                pe.wait_ge(xn_ready, b + 1)
                if b >= 2:
                    pe.wait_ge(xnT_ready, b - 1)
                for q in range(TPB):
                    ins = T.transpose(ps[:, b % 2, P * q:P * (q + 1)], xn[:, b * TPB + q, 0:DM], ident)
                ins.then_inc(xT_psum, 1)

            turn(0)
            for b in range(BATCH):
                if b + 1 < BATCH:
                    turn(b + 1)
                pe.wait_ge(xT_ready, b + 1)
                if b >= 2:
                    pe.wait_ge(vr_used, 2 * (b - 1))
                for q in range(TPB):
                    ins = T.matmul(ps[:, 2 + b % 2, VR * q:VR * (q + 1)], xT[:, b % 2, P * q:P * (q + 1)], wvr[:],
                                   start=True, stop=True)
                ins.then_inc(vr_psum, 1)

            pe.wait_ge(xnT_ready, BATCH)
            pe.wait_ge(vr_used, 2 * BATCH)
            for b in range(BATCH + 1):
                if b < BATCH:
                    if b >= 2:
                        pe.wait_ge(q_neg_ready, b - 1)
                    T.matmul(ps[:, 5 + b % 2, :], wqp[:], xnT[:, b * SEQ:(b + 1) * SEQ], start=True, stop=True)\
                     .then_inc(q_psum, 1)
                if b == 1:
                    pe.wait_ge(sums_ready, 1)
                    T.matmul(ps[:, 4, 0:8], below, row_sum, start=True, stop=True)
                    T.matmul(ps[:, 4, 8:16], ones, row_sum, start=True, stop=True).then_inc(sums_psum, 1)
                if b >= 1:
                    pe.wait_ge(sigma_ready, b)
                    if b >= 3:
                        pe.wait_ge(mem_used, b - 2)
                    k = (b - 1) % 2
                    for q in range(TPB):
                        c = 256 * (q % 2)
                        ins = T.matmul(ps[:, 2 * k + q // 2, c:c + 2 * MEMW], sigma[:, P * q:P * (q + 1)],
                                       memb[:], start=True, stop=True)
                    ins.then_inc(mem_psum, 1)

            def keys(st, b):
                T.matmul(ps[:, 7, :], wks[:, st % 4, :], xnT[:, bass.ts(b, SEQ)], start=True, stop=True).then_inc(ka_psum, 1)

            def queries(st, b):
                T.matmul(ps[:, 7, :], wqs[:, st % 4, :], xnT[:, bass.ts(b, SEQ)], start=True, stop=True).then_inc(qa_psum, 1)

            def probabilities(st, u, c, js):
                for j in js:
                    n = 4 * c + j
                    if st >= 1 or n >= 2:
                        pe.wait_ge(p_ready, u * 16 + (n - 1))
                    T.matmul(ps[:, 4 + n % 2, :], k_zero[:, st % 4, j, P * c:P * (c + 1)],
                             q_stack[:, st % 4, :], start=True, stop=True).then_inc(st_psum, 1)

            def scores(st, t, c, js):
                for j in js:
                    n = 4 * c + j
                    if st >= 1 or n >= 2:
                        pe.wait_ge(max_ready, t * 16 + (n - 1))
                    T.matmul(ps[:, j % 2, :], q_stack[:, st % 4, P * c:P * (c + 1)],
                             k_zero[:, st % 4, j, :], start=True, stop=True).then_inc(s_psum, 1)

            def sums(st, u, c):
                if c == 0:
                    pe.wait_ge(v_ready, u + 1)
                    if st >= 1:
                        pe.wait_ge(pv_copied, u)
                pe.wait_ge(p_ready, u * 16 + (4 * c + 4))
                for j in range(4):
                    v0 = VW * (j // 2)
                    ins = T.matmul(ps[32 * j:32 * j + 32, 6, :], v_unit[:, st % 4, c, v0:v0 + 32],
                                   probs[:, 4 * (c % 2) + j, :], start=(c == 0), stop=(c == 3))
                ins.then_inc(pv_psum, 1)

            def step(st, t, batch, half):
                a_on, b_on, m_on, c_on, o_on = (has_unit(st + d) for d in (1, 0, -1, -2, -3))
                if c_on:
                    pe.wait_ge(m_rows, (t - 1) * 32)
                if b_on:
                    pe.wait_ge(kz_ready[st % 2], half(2) * 64)
                    pe.wait_ge(qs_ready, t + 1)
                for c in range(4):
                    if c_on:
                        probabilities(st - 2, t - 2, c, (0, 1))
                    if b_on:
                        scores(st, t, c, (0, 1))
                    if c == 0 and a_on:
                        if has_unit(st - 4):
                            pe.wait_ge(att_ready, t - 3)
                        else:
                            pe.wait_ge(qs_ready, t + 1)
                        keys(st + 1, batch(1))
                    if c == 1 and m_on:
                        pe.wait_ge(max_ready, t * 16)
                        if a_on:
                            pe.wait_ge(ks_ready, t + 2)
                        elif has_unit(st - 4):
                            pe.wait_ge(att_ready, t - 3)
                        T.transpose(ps[0:16, 7, 0:P], neg_max[:, (st - 1) % 2, :], ident).then_inc(mt_psum, 1)
                    if c == 2 and a_on:
                        if m_on:
                            pe.wait_ge(m_ready, t)
                        else:
                            pe.wait_ge(ks_ready, t + 2)
                        queries(st + 1, batch(1))
                    if c == 3 and o_on:
                        pe.wait_ge(pv_copied, t - 2)
                        if a_on:
                            pe.wait_ge(qs_ready, t + 2)
                        elif m_on:
                            pe.wait_ge(m_ready, t)
                        else:
                            pe.wait_ge(att_ready, t - 3)
                        for q in range(TPB):
                            ins = T.transpose(ps[:, 7, P * q:P * (q + 1)], pv_sb[:, P * q:P * (q + 1)], ident)
                        ins.then_inc(o_psum, 1)
                    if c == 1 and has_block(st - 5):
                        pe.wait_ge(y_copied, t - 4)
                        for q in range(4):
                            ins = T.transpose(ps[:, 3, P * q:P * (q + 1)], y_sb[:, P * q:P * (q + 1)], ident)
                        ins.then_inc(yt_psum, 1)
                    if c == 2 and has_block(st - 4):
                        pe.wait_ge(block_in[st % 2], half(-2) * 48)
                        if st > FIRST_BLOCK:
                            pe.wait_ge(y_copied, t - 4)
                        for q in range(4):
                            ins = T.transpose(ps[:, 2, P * q:P * (q + 1)], x_rows[:, st % 2, q, 0:DM], ident)
                        ins.then_inc(xt_psum, 1)
                    if c_on:
                        probabilities(st - 2, t - 2, c, (2, 3))
                    if b_on:
                        scores(st, t, c, (2, 3))
                    if c == 0 and o_on:
                        sums(st - 3, t - 3, 3)
                    if c >= 1 and c_on:
                        sums(st - 2, t - 2, c - 1)

                if has_block(st - 4):
                    pe.wait_ge(w_split, t - 3)
                    pe.wait_ge(x_lo_ready, t - 3)
                    if st > FIRST_BLOCK:
                        pe.wait_ge(yt_ready, t - 4)
                    for f in range(FT):
                        if f >= 2:
                            pe.wait_ge(h_ready, t * 4 + (f - 17))
                        w = slice(P * f, P * (f + 1))
                        T.matmul(ps[:, 2 + f % 2, :], w_hi[:, w], x_hi[:], start=True, stop=False)
                        T.matmul(ps[:, 2 + f % 2, :], w_hi[:, w], x_lo[:], start=False, stop=False)
                        T.matmul(ps[:, 2 + f % 2, :], w_lo[:, w], x_hi[:], start=False, stop=True).then_inc(h_psum, 1)
                    pe.wait_ge(h_ready, t * 4 - 13)
                    for f in range(FT):
                        w = slice(FF + P * f, FF + P * (f + 1))
                        pe.wait_ge(h_lo_ready, t * 4 + (f - 15))
                        T.matmul(ps[:, 2, :], w_hi[:, w], h_hi[:, f, :], start=(f == 0), stop=False)
                        T.matmul(ps[:, 2, :], w_hi[:, w], h_lo[:, f, :], start=False, stop=False)
                        ins = T.matmul(ps[:, 2, :], w_lo[:, w], h_hi[:, f, :], start=False, stop=(f == FT - 1))
                    ins.then_inc(y_psum, 1)

            keys(0, 0)
            pe.wait_ge(ks_ready, 1)
            queries(0, 0)
            pe.wait_ge(mem_used, BATCH)
            unit_loop(pe, step)


def kernel(**inputs):
    import concourse.bacc as bacc
    from concourse.bass_utils import run_bass_kernel_spmd

    a = {k[3:]: np.ascontiguousarray(v) for k, v in inputs.items()}
    f32 = a["attn_x"].dtype
    wq_stack = np.zeros((DM, GROUPS, 4, 4, DH), f32)
    wk_stack = np.zeros((DM, GROUPS, 4, 4, DH), f32)
    for h in range(HEADS):
        for part in range(3):
            kv = h // (HEADS // KVH)
            wq_stack[:, h // 4, h % 4, part] = a["attn_Wq"][:, h * DH:(h + 1) * DH]
            wk_stack[:, h // 4, h % 4, part] = a["attn_Wk"][:, kv * DH:(kv + 1) * DH]
    wv_router = np.zeros((DM, VCOLS + EXPERTS), f32)
    for kv in range(KVH):
        wv_router[:, kv * VW:kv * VW + DH] = a["attn_Wv"][:, kv * DH:(kv + 1) * DH]
    wv_router[:, VCOLS:] = a["ffn_router_w"].T
    mem_block = np.zeros((DM, 2 * MEMW), f32)
    for g in range(2):
        mem_block[64 * g:64 * g + 64, MEMW * g:MEMW * g + 64] = a["attn_memory"]
        mem_block[64 * g:64 * g + 64, MEMW * g + 64] = a["attn_memory_norm"]
    row = np.arange(P) % 32
    consts = np.zeros((P, C_ALL), f32)
    consts[:, C_IDENT:C_IDENT + P] = np.eye(P)
    consts[:, C_BELOW:C_BELOW + P] = np.triu(np.ones((P, P)), 1)
    consts[:, C_ONES:C_ONES + P] = 1.0
    consts[:, C_IOTA:C_IOTA + EXPERTS] = np.arange(EXPERTS)
    consts[:, C_FILL:C_FILL + 8] = BS * np.arange(8)
    consts[:, C_BLOCK:C_BLOCK + BLOCKS] = np.arange(BLOCKS)
    consts[:, C_NEXT:C_NEXT + EXPERTS * TILES] = np.arange(EXPERTS * TILES) % TILES > 0
    consts[(row >= 16) & (row < 24), C_QSIGN] = -1.0
    consts[(row >= 8) & (row < 16), C_KSIGN] = -1.0
    consts[(row == 24) | (row == 25), C_KSIGN] = 1.0
    consts[(row == 24) | (row == 25), C_KONE] = 1.0
    w_experts = np.zeros((EXPERTS, P, 2 * FF), f32)
    w_experts[:, :, 0:FF] = a["ffn_w1"].transpose(0, 2, 1)
    w_experts[:, :, FF:] = a["ffn_w2"].reshape(EXPERTS, DM, FT, P).transpose(0, 3, 2, 1).reshape(EXPERTS, P, FF)
    b_experts = np.zeros((EXPERTS, P, FT + 1), f32)
    b_experts[:, :, 0:FT] = a["ffn_b1"].reshape(EXPERTS, FT, P).transpose(0, 2, 1)
    b_experts[:, :, FT] = a["ffn_b2"]
    arrays = {
        "x": a["attn_x"],
        "wq_stack": wq_stack.reshape(DM, GROUPS, P),
        "wk_stack": wk_stack.reshape(DM, GROUPS, P),
        "wq": a["attn_Wq"],
        "wv_router": wv_router,
        "mem_block": mem_block,
        "mem_weight": a["attn_memory_weight"],
        "w_experts": w_experts,
        "b_experts": b_experts,
        "consts": consts,
    }
    nc = bacc.Bacc("TRN2", target_bir_lowering=False, num_devices=1)
    args = [nc.dram_tensor(f"in_{k}", v.shape, mybir.dt.from_np(v.dtype), kind="ExternalInput").ap()
            for k, v in arrays.items()]
    out = nc.dram_tensor("out", arrays["x"].shape, F32, kind="ExternalOutput").ap()
    build(nc, *args, out)
    r = run_bass_kernel_spmd(nc, [{f"in_{k}": v for k, v in arrays.items()}], core_ids=[0])
    return r.results[0]["out"]
```

```python
from contextlib import ExitStack

import numpy as np

import concourse.bass as bass
from concourse import mybir

F32 = mybir.dt.float32
F32R = mybir.dt.float32r
U32 = mybir.dt.uint32
I32 = mybir.dt.int32
ALU = mybir.AluOpType
ACT = mybir.ActivationFunctionType
AX = mybir.AxisListType

P = 128
BATCH, SEQ, DM = 8, 512, 128
HEADS, DH, KVH = 16, 8, 8
TILES = BATCH * SEQ // P
TPB = SEQ // P
GROUPS = 4
UNITS = BATCH * GROUPS
EXPERTS, FF, TOP = 8, 512, 2
FT = FF // P
BS = 512
HS = BS // 2
HALVES = (TOP * BATCH * SEQ + EXPERTS * (HS - 1)) // HS
BLOCKS = (HALVES + 1) // 2
FILLS = BATCH * SEQ // HS
XW = DM + 1
VW = DH + 1
VCOLS = KVH * VW
VR = VCOLS + EXPERTS
MEMW = 65
LN_EPS = 1e-5
SCALE = 1.0 / float(np.sqrt(DH))
STEPS = UNITS + 2
FIRST_BLOCK = 4
POOL_TILES = (1, 3)
PARTS = 3
KR = PARTS * DH
HL = 2 * DH
QR = KR + 2

C_IDENT, C_BELOW, C_ONES = 0, P, 2 * P
C_IOTA, C_FILL, C_HALF = 3 * P, 3 * P + 8, 3 * P + 8 + FILLS
C_NEXT = C_HALF + 2 * BLOCKS
C_KONE = C_NEXT + EXPERTS * TILES
C_ALL = C_KONE + 1


def front_loop(eng, step, extra):
    for b in range(2):
        step(b, b, b // 2)
    with eng.Fori(0, 2) as i:
        for s in (2, 3):
            step(s, i * 2 + s, i + s // 2)
    for b in range(6, BATCH + extra):
        step(b, b, b // 2)


def unit_loop(eng, step):
    first, last = 8, 20
    for t in range(first):
        step(t, t, lambda k: (t + k) // 4, lambda k: (t + k) // 2)
    with eng.Fori(0, (last - first) // 4) as i:
        for s in range(first, first + 4):
            step(s, i * 4 + s, lambda k: i + (s + k) // 4, lambda k: i * 2 + (s + k) // 2)
    for t in range(last, STEPS):
        step(t, t, lambda k: (t + k) // 4, lambda k: (t + k) // 2)


def has_unit(u):
    return 0 <= u < UNITS


def has_block(n):
    return 0 <= n < BLOCKS


def no_block(st):
    return not (has_block(st - FIRST_BLOCK) or has_block(st - FIRST_BLOCK - 1))


def score_bank(u, n):
    return (4, 5, 2, 3)[n % 4] if no_block(u + 1) else 4 + n % 2


def max_bank(u, n):
    return n % 4 if u == 0 else n % 2


def build(nc, x, wq, wk, wv_router, mem_block, mem_weight, w_experts, b_experts, consts_in, out):
    ctx = ExitStack()
    with ctx:
        def sb(name, shape, dt=F32):
            return ctx.enter_context(nc.sbuf_tensor(name, shape, dt))

        def sem(name):
            return ctx.enter_context(nc.semaphore(name))

        x_slots = nc.dram_tensor("x_slots", [BLOCKS * BS, XW], F32, kind="Internal").ap()
        y_slots = nc.dram_tensor("y_slots", [BLOCKS * BS, DM], F32, kind="Internal").ap()

        q_rows = nc.dram_tensor("q_rows", [UNITS * 4, HL + 2, SEQ], F32, kind="Internal").ap()
        k_rows = nc.dram_tensor("k_rows", [BATCH * KVH, HL, SEQ], F32, kind="Internal").ap()

        consts = sb("consts", [P, C_ALL])
        ident = consts[:, C_IDENT:C_IDENT + P]
        below = consts[:, C_BELOW:C_BELOW + P]
        ones = consts[:, C_ONES:C_ONES + P]
        iota = consts[:, C_IOTA:C_IOTA + EXPERTS]
        fills = consts[:, C_FILL:C_FILL + FILLS]
        half_no = consts[:, C_HALF:C_HALF + 2 * BLOCKS]
        carry = consts[:, C_NEXT:C_NEXT + EXPERTS * TILES]
        k_one = consts[:, C_KONE:C_KONE + 1]
        xs = sb("xs", [P, TILES, DM])
        xn = sb("xn", [P, TILES, XW])
        xnT = sb("xnT", [P, BATCH * SEQ])
        att = sb("att", [P, TILES, DM])
        values = sb("values", [P, TILES, VCOLS])
        logits = sb("logits", [P, TILES, EXPERTS])
        wqp = sb("wqp", [P, DM])
        wkp = sb("wkp", [P, KVH * DH])
        wvr = sb("wvr", [P, VR])
        memb = sb("memb", [P, 2 * MEMW])
        mw = sb("mw", [P, 1])
        tanh_w = sb("tanh_w", [P, 1])
        w_mem = sb("w_mem", [P, 1])
        w_dot = sb("w_dot", [P, 1])
        eps = sb("eps", [P, 1])
        warm = sb("warm", [P, 2])
        stats = sb("stats", [P, TILES, 6])
        mv = sb("mv", [P, TILES, 2])
        std = sb("std", [P, TILES])
        rstd = sb("rstd", [P, TILES])
        mden = sb("mden", [P, TPB, 2])
        q_split = sb("q_split", [P, 2, 2, SEQ], F32R)
        k_split = sb("k_split", [KVH * DH, 2, 2, SEQ], F32R)
        q_stack = sb("q_stack", [P, 4, SEQ], F32R)
        k_zero = sb("k_zero", [P, 2, 4, SEQ], F32R)
        v_pair = sb("v_pair", [P, 2, TPB, 4 * VW + 23])
        neg_max = sb("neg_max", [P, 2, 16])
        m_hi = sb("m_hi", [16, P], F32R)
        m_lo = sb("m_lo", [16, P], F32R)
        probs = sb("probs", [P, 8, SEQ])
        pv_sb = sb("pv_sb", [P, SEQ])
        rden = sb("rden", [P, TPB, 4])
        o_tmp = sb("o_tmp", [P, TPB, 4, DH])
        scratch = sb("scratch", [P, 6152])
        w_raw = scratch[:, 0:2048].rearrange("p (h w) -> p h w", h=2)
        x_rows = scratch[:, 2048:2048 + 2 * 4 * XW].rearrange("p (b q d) -> p b q d", b=2, q=4)
        h_f32 = scratch[:, 3080:3080 + 2048].rearrange("p (b s) -> p b s", b=4)
        y_sb = scratch[:, 5128:5128 + BS]
        y_rows = scratch[:, 5640:5640 + BS].rearrange("p (q d) -> p q d", q=4)
        bias = sb("bias", [P, 2, 2, FT + 1])
        w_hi = sb("w_hi", [P, 2, 2 * FF], F32R)
        w_lo = sb("w_lo", [P, 2, 2 * FF], F32R)
        x_hi = sb("x_hi", [P, BS], F32R)
        x_lo = sb("x_lo", [P, BS], F32R)
        h_hi = sb("h_hi", [P, FT, BS], F32R)
        h_lo = sb("h_lo", [P, FT, BS], F32R)
        q_neg, q_exp, q_tanh, sigma = (
            scratch[:, 1024 * k:1024 * (k + 1)].rearrange("p (b s) -> p b s", b=2) for k in range(4))
        chosen0, chosen1, chosen, upto, slot_all, prod = (
            probs[:, k // 2, 256 * (k % 2):256 * (k % 2) + 256].rearrange("p (e t) -> p e t", e=EXPERTS) for k in range(6))
        top = probs[:, 3, 0:256].rearrange("p (t e) -> p t e", e=8)
        over = probs[:, 3, 256:256 + EXPERTS * FILLS].rearrange("p (e j) -> p e j", e=EXPERTS)
        passed = probs[:, 4, 0:2 * BLOCKS * EXPERTS].rearrange("p (n e) -> p n e", e=EXPERTS)
        top_f = sb("top_f", [P, TILES, 2])
        top_i = sb("top_i", [P, TILES, 8], U32)
        gap = sb("gap", [P, TILES])
        tgap = sb("tgap", [P, TILES])
        gates = sb("gates", [P, 2, TILES])
        small = sb("small", [P, 6, 8])
        row_sum, halves_of, end_half, start_half, base = (small[:, k, :] for k in range(5))
        slot_f = sb("slot_f", [P, 2, TILES])
        slots = sb("slots", [P, 2, TILES], U32)
        expert_f = sb("expert_f", [P, 2 * BLOCKS])
        expert_of = sb("expert_of", [P, 2 * BLOCKS], I32)

        ps = ctx.enter_context(nc.psum_tensor("ps", [P, 8, SEQ], F32))

        in_w = sem("in_w")
        in_x = [sem(f"in_x{b}") for b in range(BATCH)]
        setup = sem("setup")
        zeros_stored = sem("zeros_stored")
        chain, q_chain, m_chain, r_chain, o_chain, f_chain = (
            sem(k) for k in ("chain", "q_chain", "m_chain", "r_chain", "o_chain", "f_chain"))
        var_ready, std_ready, xn_ready, mw_ready = (sem(k) for k in ("var_ready", "std_ready", "xn_ready", "mw_ready"))
        rstd_ready, xn_pool, w_ready, ones_set = (sem(k) for k in ("rstd_ready", "xn_pool", "w_ready", "ones_set"))
        xT_psum, xnT_ready = sem("xT_psum"), sem("xnT_ready")
        vr_psum, vr_used = sem("vr_psum"), sem("vr_used")
        gap_ready, tgap_ready, sums_ready, sums_psum = (
            sem(k) for k in ("gap_ready", "tgap_ready", "sums_ready", "sums_psum"))
        gates_ready, gate_placed, slots_ready, experts_ready = (
            sem(k) for k in ("gates_ready", "gate_placed", "slots_ready", "experts_ready"))
        scattered = [sem("scattered0"), sem("scattered1")]
        q_psum, q_act_ready, sigma_ready = (
            sem(k) for k in ("q_psum", "q_act_ready", "sigma_ready"))
        mem_psum, mem_used = sem("mem_psum"), sem("mem_used")
        k_psum, k_hi_ready, k_lo_ready = sem("k_psum"), sem("k_hi_ready"), sem("k_lo_ready")
        q_hi_ready, q_lo_ready = sem("q_hi_ready"), sem("q_lo_ready")
        rows_stored = [sem("rows_stored0"), sem("rows_stored1")]
        q_in = [sem(f"q_in{k}") for k in range(4)]
        k_in = [sem("k_in0"), sem("k_in1")]
        s_psum, max_ready = sem("s_psum"), sem("max_ready")
        mt_psum, m_hi_ready, m_ready, m_rows = sem("mt_psum"), sem("m_hi_ready"), sem("m_ready"), sem("m_rows")
        st_psum, p_ready = sem("st_psum"), sem("p_ready")
        v_ready = sem("v_ready")
        pv_psum, pv_copied = sem("pv_psum"), sem("pv_copied")
        o_psum, att_ready = sem("o_psum"), sem("att_ready")
        block_in = [sem("block_in0"), sem("block_in1")]
        w_hi_ready, w_split = sem("w_hi_ready"), sem("w_split")
        xt_psum, x_hi_ready, x_lo_ready = sem("xt_psum"), sem("x_hi_ready"), sem("x_lo_ready")
        h_psum, h_ready, h_hi_ready, h_lo_ready, h_lo_pool = (
            sem(k) for k in ("h_psum", "h_ready", "h_hi_ready", "h_lo_ready", "h_lo_pool"))
        y_psum, y_copied, yt_psum, yt_ready, y_stored = (
            sem(k) for k in ("y_psum", "y_copied", "yt_psum", "yt_ready", "y_stored"))
        gathered = [sem("gathered0"), sem("gathered1")]
        x_again, silu_ready, fin_ready, stored = (sem(k) for k in ("x_again", "silu_ready", "fin_ready", "stored"))

        block = ctx.enter_context(nc.Block())

        x_view = x.rearrange("b (q p) d -> p b q d", p=P)
        out_view = out.rearrange("b (q p) d -> p b q d", p=P)
        x_slot_blocks = x_slots.rearrange("(n h p q) d -> n p h (q d)", h=2, p=P, q=2)
        y_slot_blocks = y_slots.rearrange("(n h p q) d -> n p h (q d)", h=2, p=P, q=2)
        W_LOADS = 6
        BLOCK_IN = 5 * 16
        ROWS_IN = 4 * 2 * 16
        ROW_STORES = 2 * 2

        @block.sync
        def _(sp):
            sp.dma_start(consts[:], consts_in).then_inc(in_w, 16)
            for b in range(BATCH):
                sp.dma_start(xs[:, b * TPB:(b + 1) * TPB, :], x_view[:, b]).then_inc(in_x[b], 16)
                if b == 1:
                    for dst, src in ((wvr[:], wv_router), (mw[:], mem_weight.partition_broadcast(P)), (wqp[:], wq),
                                     (memb[:], mem_block), (wkp[:], wk)):
                        sp.dma_start(dst, src).then_inc(in_w, 16)
            sp.wait_ge(setup, 1)
            for n in range(BLOCKS):
                sp.dma_start(x_slot_blocks[n],
                             q_stack[:].bitcast(F32).rearrange("p j s -> p (j s)")[:, 0:4 * XW]
                             .rearrange("p (h w) -> p h w", h=2))\
                  .then_inc(zeros_stored, 16)

            sp.dma_start(q_rows[:, HL:HL + 2], q_stack[:, 0:2].bitcast(F32)).then_inc(zeros_stored, 16)

            def store_rows(st, b, half):
                sp.wait_ge(q_lo_ready, b + 1)
                sp.wait_ge(k_lo_ready, b + 1)
                for hl in range(2):
                    sp.dma_start(q_rows[bass.ds(b * 16, 16), DH * hl:DH * (hl + 1)],
                                 q_split[:, st % 2, hl, :].bitcast(F32))\
                      .then_inc(rows_stored[st % 2], 16)
                for hl in range(2):
                    sp.dma_start(k_rows[bass.ds(b * KVH, KVH), DH * hl:DH * (hl + 1)],
                                 k_split[:, st % 2, hl, :].bitcast(F32))\
                      .then_inc(rows_stored[st % 2], 16)

            def load_queries(st, u):
                for j in range(4):
                    for row, n in ((0, DH), (DH, HL + 2)):
                        sp.dma_start(q_stack[32 * j + row:32 * j + row + n, st % 4, :].bitcast(F32),
                                     q_rows[bass.ds(u * 4 + j, 1), 0:n].rearrange("a r s -> (a r) s"))\
                          .then_inc(q_in[st % 4], 16)

            def load_keys(sp_pair, pair):
                for j in range(4):
                    for row, n in ((0, HL), (HL, DH)):
                        sp.dma_start(k_zero[32 * j + row:32 * j + row + n, sp_pair % 2, j, :].bitcast(F32),
                                     k_rows[bass.ds(pair * 4 + j, 1), 0:n].rearrange("a r s -> (a r) s"))\
                          .then_inc(k_in[sp_pair % 2], 16)

            def expert(k):
                return sp.value_load(expert_of[0:1, k:k + 1] if isinstance(k, int) else expert_of[0:1, bass.ds(k, 1)],
                                     min_val=0, max_val=EXPERTS - 1)

            def load_block(st, n, experts):
                for h, e in enumerate(experts):
                    sp.dma_start(w_raw[:, h], w_experts[bass.ds(e, 1)].rearrange("a p w -> p (a w)"))\
                      .then_inc(block_in[(st - FIRST_BLOCK) % 2], 16)
                    sp.dma_start(bias[:, (st - FIRST_BLOCK) % 2, h, :],
                                 b_experts[bass.ds(e, 1)].rearrange("a p w -> p (a w)")).then_inc(block_in[(st - FIRST_BLOCK) % 2], 16)
                if st == FIRST_BLOCK:
                    for k in range(2):
                        sp.wait_ge(scattered[k], 16 * TILES)
                sp.dma_start(x_rows[:, (st - FIRST_BLOCK) % 2].rearrange("p (h q) d -> p h (q d)", h=2),
                             x_slot_blocks[n] if isinstance(n, int) else
                             x_slot_blocks[bass.ds(n, 1)].rearrange("a p h w -> p (a h) w")).then_inc(block_in[(st - FIRST_BLOCK) % 2], 16)

            def step(st, t, batch, half):
                if has_unit(st + 2):
                    if st >= 2:
                        sp.wait_ge(st_psum, (t - 1) * 16)
                    load_queries(st + 2, t + 2)
                if st == 6:
                    sp.dma_start(xnT[:].rearrange("p (b q d) -> p b q d", b=BATCH, q=TPB), x_view).then_inc(x_again, 16)
                if has_block(st - FIRST_BLOCK - 1):
                    sp.wait_ge(yt_ready, t - FIRST_BLOCK)
                    n = t - (FIRST_BLOCK + 1)
                    sp.dma_start(y_slot_blocks[n] if isinstance(t, int) else
                                 y_slot_blocks[bass.ds(n, 1)].rearrange("a p h w -> p (a h) w"),
                                 y_rows.rearrange("p (h q) d -> p h (q d)", h=2)).then_inc(y_stored, 16)
                def block():
                    if has_block(st - FIRST_BLOCK + 1):
                        if st == FIRST_BLOCK - 1:
                            sp.wait_ge(experts_ready, 1)
                        n = t - (FIRST_BLOCK - 1)
                        experts = [expert(n * 2 + h) for h in range(2)]
                        if st == FIRST_BLOCK - 1:
                            sp.wait_ge(mem_used, BATCH)
                        else:
                            sp.wait_ge(w_split, n * 2)
                        load_block(st + 1, n, experts)

                def keys():
                    if st % 2 == 0 and has_unit(st + 2):
                        if st >= 2:
                            sp.wait_ge(st_psum, t * 16)
                        load_keys((st + 2) // 2, half(2))

                def maxima_rows():
                    if has_unit(st):
                        sp.wait_ge(m_ready, t + 1)
                        for row, part in ((24, m_hi), (25, m_lo)):
                            sp.dma_start(q_stack[row:P:32, st % 4, :].bitcast(F32),
                                         part[:].bitcast(F32)).then_inc(m_rows, 16)

                if no_block(st):
                    maxima_rows()
                    block()
                else:
                    block()
                    maxima_rows()
                keys()

            def store_and_start(st, b, half):
                if st == 6:
                    sp.wait_ge(zeros_stored, 16 * (BLOCKS + 1))
                    sp.wait_ge(ones_set, 4)
                    sp.wait_ge(rows_stored[0], 16 * ROW_STORES * 3)
                    load_keys(0, 0)
                    load_queries(0, 0)
                    load_queries(1, 1)
                store_rows(st, b, half)

            front_loop(sp, store_and_start, 0)
            for k in range(2):
                sp.wait_ge(rows_stored[k], 16 * ROW_STORES * BATCH // 2)
            unit_loop(sp, step)

            for b in range(BATCH):
                sp.wait_ge(fin_ready, b + 1)
                sp.dma_start(out_view[:, b], att[:, b * TPB:(b + 1) * TPB, :]).then_inc(stored, 16)
            sp.wait_ge(stored, 16 * BATCH)

        @block.gpsimd
        def _(pool):
            pool.memset(q_stack[:].bitcast(F32), 0.0).then_inc(setup, 1)
            pool.memset(values[:], 1.0).then_inc(setup, 1)
            pool.memset(v_pair[:], 0.0).then_inc(setup, 1)
            pool.memset(k_zero[:].bitcast(F32), 0.0).then_inc(setup, 1)
            pool.wait_ge(rstd_ready, 1)
            for b in range(BATCH):
                for t in range(b * TPB + 3, (b + 1) * TPB):
                    ins = pool.tensor_scalar(xn[:, t, 0:DM], xs[:, t, :], mv[:, t, 0:1], rstd[:, t:t + 1],
                                             ALU.subtract, ALU.mult)
                ins.then_inc(xn_pool, 1)
                if b == 0:
                    pool.wait_ge(mw_ready, 1)
                    pool.tensor_scalar(w_mem[:], tanh_w[:], 0.5, 0.5, ALU.mult, ALU.add).then_inc(w_ready, 1)
                    pool.tensor_scalar(w_dot[:], tanh_w[:], -0.5, 0.5, ALU.mult, ALU.add).then_inc(w_ready, 1)
            pool.wait_ge(setup, 4)
            pool.wait_ge(vr_used, 2 * BATCH)

            def pair_values(pair, b):
                pool.tensor_copy(v_pair[:, pair % 2, :, 0:4 * VW],
                                 values[:, bass.ts(b, TPB), 4 * VW * (pair % 2):4 * VW * (pair % 2 + 1)])\
                    .then_inc(v_ready, 1)

            pair_values(0, 0)
            pool.wait_ge(zeros_stored, 16 * (BLOCKS + 1))
            for k in range(2):
                if k:
                    pool.wait_ge(scattered[0], 16 * TILES)
                else:
                    pool.wait_ge(slots_ready, 1)
                    pool.wait_ge(gates_ready, 1)
                pool.tensor_copy(xn[:, :, DM], gates[:, k, :]).then_inc(gate_placed, 1)
                pool.wait_ge(gate_placed, k + 1)
                for t in range(TILES):
                    pool.indirect_dma_start(out=x_slots, out_offset=bass.IndirectOffsetOnAxis(ap=slots[:, k, t:t + 1], axis=0),
                                            in_=xn[:, t, :], in_offset=None).then_inc(scattered[k], 16)

            def step(st, t, batch, half):
                if has_block(st - FIRST_BLOCK):
                    n = t - FIRST_BLOCK
                    pool.wait_ge(block_in[(st - FIRST_BLOCK) % 2], half(2 - FIRST_BLOCK) * BLOCK_IN)
                    for k, w in enumerate((slice(0, FF), slice(FF, 2 * FF))):
                        if st > FIRST_BLOCK:
                            if k == 0:
                                pool.wait_ge(h_psum, n * FT)
                            else:
                                pool.wait_ge(y_psum, n)
                        pool.tensor_tensor(w_hi[:, :, w], w_raw[:, :, w], ones[:, 0:1].unsqueeze(2).to_broadcast([P, 2, FF]),
                                           ALU.mult).then_inc(w_hi_ready, 1)
                        pool.wait_ge(w_hi_ready, n * 2 + (k + 1))
                        pool.tensor_tensor(w_lo[:, :, w], w_raw[:, :, w], w_hi[:, :, w].bitcast(F32), ALU.subtract)\
                            .then_inc(w_split, 1)
                    for f in POOL_TILES:
                        pool.wait_ge(h_hi_ready, n * 4 + (f + 1))
                        pool.tensor_tensor(h_lo[:, f, :], h_f32[:, f, :], h_hi[:, f, :].bitcast(F32),
                                           ALU.subtract).then_inc(h_lo_pool, 1)
                if st % 2 == 0 and has_unit(st + 2):
                    if st >= 2:
                        pool.wait_ge(pv_psum, t * TPB)
                    pair_values((st + 2) // 2, batch(2))

            def gather(k, tiles):
                for t in tiles:
                    pool.indirect_dma_start(out=xs[:, t, :], out_offset=None, in_=y_slots,
                                            in_offset=bass.IndirectOffsetOnAxis(ap=slots[:, k, t:t + 1], axis=0),
                                            compute_op=ALU.add if k else ALU.bypass).then_inc(gathered[k], 16)

            def step_and_gather(st, t, batch, half):
                step(st, t, batch, half)
                n = st - (FIRST_BLOCK + BLOCKS)
                if n == 1:
                    pool.wait_ge(y_stored, 16 * BLOCKS)
                    gather(0, range(TILES))
                if n == 3:
                    pool.wait_ge(gathered[0], 16 * TILES)
                    gather(1, range(24))
                if n == 5:
                    gather(1, range(24, TILES))

            unit_loop(pool, step_and_gather)

        @block.scalar
        def _(act):
            A = nc.scalar
            act.wait_ge(in_w, 16 * W_LOADS)
            act.wait_ge(setup, 4)
            for j in range(4):
                r = slice(32 * j, 32 * j + 32)
                A.activation(k_zero[r, :, j, :], k_zero[r, :, j, :].bitcast(F32), ACT.Identity, bias=k_one[r])\
                    .then_inc(ones_set, 1)
            act.wait_ge(var_ready, 1)
            A.activation(std[:], mv[:, :, 1], ACT.Sqrt, bias=eps[:]).then_inc(std_ready, 1)
            A.activation(tanh_w[:], mw[:], ACT.Tanh, scale=0.5).then_inc(mw_ready, 1)

            def features(st, b, half):
                if st < BATCH:
                    act.wait_ge(xT_psum, b + 1)
                    A.copy(xnT[:, bass.ts(b, SEQ)], ps[:, st % 2, :]).then_inc(xnT_ready, 1)
                if st >= 1:
                    act.wait_ge(vr_psum, b)
                    if st == 1:
                        act.wait_ge(w_ready, 2)
                        act.wait_ge(setup, 4)
                    vr = ps[:, 2 + (st - 1) % 2, 0:TPB * VR].rearrange("p (t c) -> p t c", t=TPB)
                    A.activation(values[:, bass.ts(b - 1, TPB), :].rearrange("p t (h c) -> p t h c", c=VW)[:, :, :, 0:DH],
                                 vr[:, :, 0:VCOLS].rearrange("p t (h c) -> p t h c", c=VW)[:, :, :, 0:DH],
                                 ACT.Copy, scale=w_dot[:]).then_inc(vr_used, 1)
                    A.copy(logits[:, bass.ts(b - 1, TPB), :], vr[:, :, VCOLS:VR]).then_inc(vr_used, 1)
            front_loop(act, features, 1)

            act.wait_ge(gap_ready, 1)
            A.activation(tgap[:], gap[:], ACT.Tanh, scale=0.5).then_inc(tgap_ready, 1)

            def elu(st, b, half):
                act.wait_ge(q_psum, b + 1)
                if st >= 2:
                    act.wait_ge(rows_stored[st % 2], half * (16 * ROW_STORES))
                A.copy(q_split[:, st % 2, 0, :], ps[:, 5 + st % 2, :]).then_inc(q_hi_ready, 1)
                if st >= 2:
                    act.wait_ge(sigma_ready, b - 1)
                A.activation(q_neg[:, st % 2], ps[:, 5 + st % 2, :], ACT.Relu, scale=-1.0).then_inc(q_act_ready, 1)
                act.wait_ge(k_psum, b + 1)
                A.copy(k_split[:, st % 2, 0, :], ps[0:KVH * DH, 7, :]).then_inc(k_hi_ready, 1)
                act.wait_ge(q_act_ready, b * 3 + 1)
                A.activation(q_exp[:, st % 2], q_neg[:, st % 2], ACT.Exp, scale=-1.0).then_inc(q_act_ready, 1)
                A.activation(q_tanh[:, st % 2], q_neg[:, st % 2], ACT.Tanh, scale=-0.5).then_inc(q_act_ready, 1)
            front_loop(act, elu, 0)

            def exps(st, u, c, js):
                for j in js:
                    n = 4 * c + j
                    act.wait_ge(st_psum, u * 16 + (n + 1))
                    if j == 0 and (st >= 1 or c >= 2):
                        act.wait_ge(pv_psum, u * 4 + (c - 1))
                    A.activation(probs[:, n % 8, :], ps[:, score_bank(st, n), :], ACT.Exp, scale=SCALE).then_inc(p_ready, 1)

            def step(st, t, batch, half):
                a_on, o_on = has_unit(st - 1), has_unit(st - 2)
                n = t - FIRST_BLOCK
                for c in range(4):
                    if a_on:
                        exps(st - 1, t - 1, c, (0, 1))
                    if c == 0 and o_on:
                        act.wait_ge(pv_psum, (t - 1) * 4)
                        if st - 2 >= 1:
                            act.wait_ge(o_psum, t - 2)
                        A.copy(pv_sb[:], ps[:, 6, :]).then_inc(pv_copied, 1)
                    if c == 1 and has_block(st - FIRST_BLOCK - 1):
                        act.wait_ge(y_psum, n)
                        if st - FIRST_BLOCK - 1 >= 1:
                            act.wait_ge(yt_psum, n - 1)
                        for h in range(2):
                            r = slice(HS * h, HS * (h + 1))
                            ins = A.activation(y_sb[:, r], ps[:, 2, r], ACT.Identity,
                                               bias=bias[:, (st - FIRST_BLOCK - 1) % 2, h, FT:FT + 1])
                        ins.then_inc(y_copied, 1)
                    if c == 2 and has_block(st - FIRST_BLOCK):
                        act.wait_ge(xt_psum, n + 1)
                        if st > FIRST_BLOCK:
                            act.wait_ge(y_psum, n)
                        A.copy(x_hi[:], ps[:, 2, :]).then_inc(x_hi_ready, 1)
                    if a_on:
                        exps(st - 1, t - 1, c, (2, 3))
                if has_block(st - FIRST_BLOCK):
                    A.activation(warm[:, 0:1], eps[:], ACT.Gelu)
                    for f in range(FT):
                        act.wait_ge(h_psum, n * 4 + (f + 1))
                        for h in range(2):
                            r = slice(HS * h, HS * (h + 1))
                            ins = A.activation(h_f32[:, f, r], ps[:, 2 + f % 2, r], ACT.Gelu,
                                               bias=bias[:, (st - FIRST_BLOCK) % 2, h, f:f + 1])
                        ins.then_inc(h_ready, 1)
                    A.activation(warm[:, 0:1], eps[:], ACT.Exp)
                if st == UNITS - 1:
                    A.activation(warm[:, 1:2], eps[:], ACT.Silu)
                    for k in range(TOP):
                        act.wait_ge(gathered[k], 16 * TILES)
                    for b in range(BATCH):
                        r = slice(b * TPB, (b + 1) * TPB)
                        A.activation(xs[:, r, :], xs[:, r, :], ACT.Silu).then_inc(silu_ready, 1)
                    A.activation(warm[:, 0:1], eps[:], ACT.Exp)

            unit_loop(act, step)

        @block.vector
        def _(dve):
            V = nc.vector
            V.memset(eps[:], LN_EPS)
            for b in range(BATCH):
                dve.wait_ge(in_x[b], 16)
                for t in range(b * TPB, (b + 1) * TPB):
                    V.bn_stats(stats[:, t, :], xs[:, t, :]).then_inc(chain, 1)
            dve.wait_ge(chain, TILES)
            for t in range(TILES):
                ins = V.bn_aggr(mv[:, t, :], stats[:, t, :])
            ins.then_inc(var_ready, 1)
            dve.wait_ge(std_ready, 1)
            V.reciprocal(rstd[:], std[:]).then_inc(rstd_ready, 1)
            dve.wait_ge(rstd_ready, 1)
            for b in range(BATCH):
                for t in range(b * TPB, b * TPB + 3):
                    ins = V.tensor_scalar(xn[:, t, 0:DM], xs[:, t, :], mv[:, t, 0:1], rstd[:, t:t + 1],
                                          ALU.subtract, ALU.mult)
                ins.then_inc(xn_ready, 1)

            count = [0]

            def link(ins, wait=True):
                count[0] += 1
                ins.then_inc(r_chain, 1)
                if wait:
                    dve.wait_ge(r_chain, count[0])

            def wide(ap, axis):
                return ap.unsqueeze(axis).to_broadcast([P, EXPERTS, TILES])

            for t in range(TILES):
                if t % TPB == 0:
                    dve.wait_ge(vr_used, 2 * (t // TPB + 1))
                link(V.max(top[:, t, :], logits[:, t, :]), wait=False)
            dve.wait_ge(r_chain, count[0])
            V.tensor_tensor(gap[:], top[:, :, 0], top[:, :, 1], ALU.subtract).then_inc(gap_ready, 1)
            for t in range(TILES):
                link(V.max_index(top_i[:, t, :], top[:, t, :], logits[:, t, :]), wait=False)
            dve.wait_ge(r_chain, count[0])
            link(V.tensor_copy(top_f[:], top_i[:, :, 0:2]))
            link(V.tensor_tensor(chosen0, wide(iota, 2), wide(top_f[:, :, 0], 1), ALU.is_equal), wait=False)
            link(V.tensor_tensor(chosen1, wide(iota, 2), wide(top_f[:, :, 1], 1), ALU.is_equal))
            link(V.tensor_tensor(chosen, chosen0, chosen1, ALU.add))
            flat = "p e t -> p (e t)"
            link(V.tensor_tensor_scan(upto.rearrange(flat), carry, chosen.rearrange(flat), 0.0, ALU.mult, ALU.add))
            V.tensor_copy(row_sum, upto[:, :, TILES - 1]).then_inc(sums_ready, 1)
            dve.wait_ge(tgap_ready, 1)
            link(V.tensor_scalar(gates[:, 0, :], tgap[:], 0.5, 0.5, ALU.mult, ALU.add), wait=False)
            V.tensor_scalar(gates[:, 1, :], tgap[:], -0.5, 0.5, ALU.mult, ALU.add).then_inc(gates_ready, 1)
            dve.wait_ge(sums_psum, 1)
            below_sum, all_sum = ps[:, 4, 0:8], ps[:, 4, 8:16]
            grid = [P, EXPERTS, FILLS]
            link(V.tensor_tensor(over, all_sum.unsqueeze(2).to_broadcast(grid), fills.unsqueeze(1).to_broadcast(grid), ALU.is_gt))
            link(V.tensor_reduce(halves_of, over, AX.X, ALU.add))
            link(V.tensor_tensor_scan(end_half, ones[:, 0:8], halves_of, 0.0, ALU.mult, ALU.add))
            link(V.tensor_tensor(start_half, end_half, halves_of, ALU.subtract), wait=False)
            grid = [P, 2 * BLOCKS, EXPERTS]
            link(V.tensor_tensor(passed, end_half.unsqueeze(1).to_broadcast(grid), half_no.unsqueeze(2).to_broadcast(grid),
                                 ALU.is_le))
            link(V.scalar_tensor_tensor(out=base, in0=start_half, scalar=float(HS), in1=below_sum,
                                        op0=ALU.mult, op1=ALU.add), wait=False)
            link(V.tensor_reduce(expert_f[:], passed, AX.X, ALU.add), wait=False)
            link(V.tensor_tensor(slot_all, upto, chosen, ALU.subtract))
            link(V.tensor_tensor(slot_all, slot_all, wide(base, 2), ALU.add), wait=False)
            V.tensor_scalar(expert_of[:], expert_f[:], float(EXPERTS - 1), None, ALU.min).then_inc(experts_ready, 1)
            dve.wait_ge(r_chain, count[0])
            for k, pick in ((0, chosen0), (1, chosen1)):
                link(V.tensor_tensor(prod, pick, slot_all, ALU.mult))
                link(V.tensor_reduce(slot_f[:, k, :], prod.rearrange("p e t -> p t e"), AX.X, ALU.add))
            V.tensor_copy(slots[:], slot_f[:]).then_inc(slots_ready, 1)

            def memory(st, b, half):
                if st < BATCH:
                    dve.wait_ge(q_act_ready, b * 3 + 1)
                    dve.wait_ge(q_hi_ready, b + 1)
                    if st >= 2:
                        dve.wait_ge(rows_stored[st % 2], half * (16 * ROW_STORES))
                    V.tensor_tensor(q_split[:, st % 2, 1, :], ps[:, 5 + st % 2, :],
                                    q_split[:, st % 2, 0, :].bitcast(F32), ALU.subtract).then_inc(q_lo_ready, 1)
                    dve.wait_ge(k_hi_ready, b + 1)
                    V.tensor_tensor(k_split[:, st % 2, 1, :], ps[0:KVH * DH, 7, :],
                                    k_split[:, st % 2, 0, :].bitcast(F32), ALU.subtract).then_inc(k_lo_ready, 1)
                if st >= 1:
                    dve.wait_ge(mem_psum, b)
                    k = (st - 1) % 2
                    num = ps[:, 2 * k:2 * k + 2, :].rearrange("p a (c n) -> p (a c) n", c=2)
                    V.reciprocal(mden[:], num[:, :, MEMW - 1:2 * MEMW:MEMW]).then_inc(m_chain, 1)
                    dve.wait_ge(m_chain, b)
                    for g in range(2):
                        ins = V.scalar_tensor_tensor(out=att[:, bass.ts(b - 1, TPB), 64 * g:64 * g + 64],
                                                     in0=num[:, :, MEMW * g:MEMW * g + 64], scalar=w_mem[:],
                                                     in1=mden[:, :, g:g + 1].to_broadcast([P, TPB, 64]),
                                                     op0=ALU.mult, op1=ALU.mult)
                    ins.then_inc(mem_used, 1)
                if st < BATCH:
                    dve.wait_ge(q_act_ready, b * 3 + 3)
                    V.scalar_tensor_tensor(out=q_exp[:, st % 2], in0=q_exp[:, st % 2], scalar=1.0, in1=q_tanh[:, st % 2],
                                           op0=ALU.add, op1=ALU.mult).then_inc(q_chain, 1)
                    dve.wait_ge(q_chain, b + 1)
                    if st >= 2:
                        dve.wait_ge(mem_psum, b - 1)
                    V.scalar_tensor_tensor(out=sigma[:, st % 2], in0=ps[:, 5 + st % 2, :], scalar=0.0,
                                           in1=q_exp[:, st % 2], op0=ALU.max, op1=ALU.add).then_inc(sigma_ready, 1)
            dve.wait_ge(w_ready, 2)
            front_loop(dve, memory, 1)

            def maxima(st, t, ns):
                for n in ns:
                    c, j = n // 4, n % 4
                    dve.wait_ge(s_psum, t * 16 + (n + 1))
                    if n == 0 and st >= 2:
                        dve.wait_ge(mt_psum, t - 1)
                    V.tensor_reduce(neg_max[:, st % 2, 4 * j + c:4 * j + c + 1], ps[:, max_bank(st, n), :],
                                    AX.X, ALU.max, negate=True).then_inc(max_ready, 1)

            def step(st, t, batch, half):
                n = t - FIRST_BLOCK
                b_on, f_on = has_unit(st + 1), has_block(st - FIRST_BLOCK)

                def turned_maxima():
                    dve.wait_ge(mt_psum, t + 1)
                    if st >= 1:
                        dve.wait_ge(m_rows, t * 32)
                    V.tensor_copy(m_hi[:], ps[0:16, 7, 0:P]).then_inc(m_hi_ready, 1)
                    dve.wait_ge(m_hi_ready, t + 1)
                    V.tensor_tensor(m_lo[:], ps[0:16, 7, 0:P], m_hi[:].bitcast(F32), ALU.subtract).then_inc(m_ready, 1)

                for c in range(4):
                    if no_block(st):
                        if c < 3 and has_unit(st):
                            maxima(st, t, range(4 + 4 * c, 6 + 4 * c))
                        if c == 3 and has_unit(st):
                            turned_maxima()
                        if c == 3 and b_on:
                            maxima(st + 1, t + 1, (0,))
                    elif has_unit(st):
                        maxima(st, t, (4 + 3 * c,))
                    if c == 1 and has_unit(st - 2):
                        dve.wait_ge(o_psum, t - 1)
                        g, b = (st - 2) % 4, batch(-2)
                        o = ps[:, 7, :].rearrange("p (t j d) -> p t j d", t=TPB, j=4)
                        V.reciprocal(rden[:], o[:, :, :, DH]).then_inc(o_chain, 1)
                        dve.wait_ge(o_chain, t * 2 - 3)
                        V.tensor_tensor(o_tmp[:], o[:, :, :, 0:DH], rden[:].unsqueeze(3).to_broadcast([P, TPB, 4, DH]),
                                        ALU.mult).then_inc(o_chain, 1)
                        dve.wait_ge(o_chain, t * 2 - 2)
                        part = att[:, bass.ts(b, TPB), 64 * (g // 2):64 * (g // 2) + 64]\
                            .rearrange("p t (j r d) -> p t j r d", j=4, r=2)[:, :, :, g % 2, :]
                        V.tensor_tensor(part, part, o_tmp[:], ALU.add).then_inc(att_ready, 1)
                    if c == 2 and has_block(st - FIRST_BLOCK - 1):
                        dve.wait_ge(yt_psum, n)
                        if st - FIRST_BLOCK - 1 >= 1:
                            dve.wait_ge(y_stored, (n - 1) * 16)
                        V.tensor_tensor(y_rows, ps[:, 3, :].rearrange("p (q d) -> p q d", q=4),
                                        x_rows[:, (st - FIRST_BLOCK - 1) % 2, :, DM:XW].to_broadcast([P, 4, DM]), ALU.mult)\
                         .then_inc(yt_ready, 1)
                    if c == 3 and has_block(st - FIRST_BLOCK):
                        dve.wait_ge(x_hi_ready, n + 1)
                        V.tensor_tensor(x_lo[:], ps[:, 2, :], x_hi[:].bitcast(F32), ALU.subtract).then_inc(x_lo_ready, 1)
                    if no_block(st):
                        if c < 3 and has_unit(st):
                            maxima(st, t, range(6 + 4 * c, 8 + 4 * c))
                        if c == 3 and b_on:
                            maxima(st + 1, t + 1, (1, 2, 3))
                    elif has_unit(st):
                        maxima(st, t, (5 + 3 * c, 6 + 3 * c))
                if no_block(st):
                    return

                def hidden(f):
                    dve.wait_ge(h_ready, n * 4 + (f + 1))
                    V.tensor_copy(h_hi[:, f, :], h_f32[:, f, :]).then_inc(h_hi_ready, 1)
                    if f not in POOL_TILES:
                        dve.wait_ge(h_hi_ready, n * 4 + (f + 1))
                        V.tensor_tensor(h_lo[:, f, :], h_f32[:, f, :], h_hi[:, f, :].bitcast(F32),
                                        ALU.subtract).then_inc(h_lo_ready, 1)

                if has_unit(st):
                    turned_maxima()
                if b_on:
                    maxima(st + 1, t + 1, (0, 1))
                if f_on:
                    if st > FIRST_BLOCK:
                        dve.wait_ge(y_psum, n)
                    hidden(0)
                    hidden(1)
                if b_on:
                    maxima(st + 1, t + 1, (2,))
                if f_on:
                    hidden(2)
                    hidden(3)
                if b_on:
                    maxima(st + 1, t + 1, (3,))
            def finish(b):
                r = slice(b * TPB, (b + 1) * TPB)
                dve.wait_ge(silu_ready, b + 1)
                V.tensor_tensor(att[:, r, :], att[:, r, :], xs[:, r, :], ALU.mult).then_inc(f_chain, 1)
                dve.wait_ge(f_chain, b + 1)
                V.tensor_tensor(att[:, r, :], att[:, r, :], xnT[:].rearrange("p (t d) -> p t d", d=DM)[:, r, :],
                                ALU.add).then_inc(fin_ready, 1)

            def step_and_finish(st, t, batch, half):
                if st == STEPS - 1:
                    dve.wait_ge(x_again, 16)
                    dve.wait_ge(att_ready, UNITS - 1)
                    for b in range(BATCH - 1):
                        finish(b)
                step(st, t, batch, half)

            maxima(0, 0, range(4))
            unit_loop(dve, step_and_finish)
            dve.wait_ge(att_ready, UNITS)
            finish(BATCH - 1)

        @block.tensor
        def _(pe):
            T = nc.tensor
            pe.wait_ge(in_w, 16 * W_LOADS)

            def turn(b):
                pe.wait_ge(xn_ready, b + 1)
                pe.wait_ge(xn_pool, b + 1)
                if b >= 2:
                    pe.wait_ge(xnT_ready, b - 1)
                for q in range(TPB):
                    ins = T.transpose(ps[:, b % 2, P * q:P * (q + 1)], xn[:, b * TPB + q, 0:DM], ident)
                ins.then_inc(xT_psum, 1)

            turn(0)
            for b in range(BATCH):
                if b + 1 < BATCH:
                    turn(b + 1)
                pe.wait_ge(xnT_ready, b + 1)
                if b >= 2:
                    pe.wait_ge(vr_used, 2 * (b - 1))
                for q in range(TPB):
                    ins = T.matmul(ps[:, 2 + b % 2, VR * q:VR * (q + 1)], xnT[:, b * SEQ + P * q:b * SEQ + P * (q + 1)], wvr[:],
                                   start=True, stop=True)
                ins.then_inc(vr_psum, 1)

            pe.wait_ge(xnT_ready, BATCH)
            pe.wait_ge(vr_used, 2 * BATCH)
            for b in range(BATCH + 1):
                if b < BATCH:
                    if b >= 2:
                        pe.wait_ge(sigma_ready, b - 1)
                    T.matmul(ps[:, 5 + b % 2, :], wqp[:], xnT[:, b * SEQ:(b + 1) * SEQ], start=True, stop=True)\
                     .then_inc(q_psum, 1)
                    if b >= 1:
                        pe.wait_ge(k_lo_ready, b)
                    T.matmul(ps[0:KVH * DH, 7, :], wkp[:], xnT[:, b * SEQ:(b + 1) * SEQ], start=True, stop=True)\
                     .then_inc(k_psum, 1)
                if b == 0:
                    pe.wait_ge(sums_ready, 1)
                    T.matmul(ps[:, 4, 0:8], below, row_sum, start=True, stop=True)
                    T.matmul(ps[:, 4, 8:16], ones, row_sum, start=True, stop=True).then_inc(sums_psum, 1)
                if b >= 1:
                    pe.wait_ge(sigma_ready, b)
                    if b >= 3:
                        pe.wait_ge(mem_used, b - 2)
                    k = (b - 1) % 2
                    for q in range(TPB):
                        c = 256 * (q % 2)
                        ins = T.matmul(ps[:, 2 * k + q // 2, c:c + 2 * MEMW], sigma[:, (b - 1) % 2, P * q:P * (q + 1)],
                                       memb[:], start=True, stop=True)
                    ins.then_inc(mem_psum, 1)

            def probabilities(st, u, c, js):
                for j in js:
                    n = 4 * c + j
                    if not no_block(st + 1):
                        pe.wait_ge(p_ready, u * 16 + (n - 1))
                    elif n >= 4 or (st >= 1 and no_block(st)):
                        pe.wait_ge(p_ready, u * 16 + (n - 3))
                    elif st >= 1 and n < 2:
                        pe.wait_ge(p_ready, u * 16 + (n - 1))
                    elif st >= 1:
                        pe.wait_ge(yt_ready, BLOCKS)
                    T.matmul(ps[:, score_bank(st, n), :], k_zero[:, (st // 2) % 2, j, P * c:P * (c + 1)],
                             q_stack[:, st % 4, :], start=True, stop=True).then_inc(st_psum, 1)

            def scores(st, t, ns):
                for n in ns:
                    c, j = n // 4, n % 4
                    if st >= 1:
                        pe.wait_ge(max_ready, t * 16 + (n - 1))
                    elif n >= 4:
                        pe.wait_ge(max_ready, n - 3)
                    T.matmul(ps[:, max_bank(st, n), :], q_stack[:, st % 4, P * c:P * (c + 1)],
                             k_zero[:, (st // 2) % 2, j, :], start=True, stop=True).then_inc(s_psum, 1)

            def sums(st, u, c, pairs):
                if c == 0:
                    if st % 2 == 0:
                        pe.wait_ge(v_ready, pairs)
                    if st >= 1:
                        pe.wait_ge(pv_copied, u)
                pe.wait_ge(p_ready, u * 16 + (4 * c + 4))
                for j in range(4):
                    ins = T.matmul(ps[32 * j:32 * j + 32, 6, :], v_pair[:, (st // 2) % 2, c, VW * j:VW * j + 32],
                                   probs[:, 4 * (c % 2) + j, :], start=(c == 0), stop=(c == 3))
                ins.then_inc(pv_psum, 1)

            def step(st, t, batch, half):
                a_on, s_on, o_on, b_on = (has_unit(st + d) for d in (-1, 0, -2, 1))
                y_on, f_on = has_block(st - FIRST_BLOCK - 1), has_block(st - FIRST_BLOCK)
                n = t - FIRST_BLOCK

                def hidden(f):
                    if f >= 2:
                        pe.wait_ge(h_ready, n * 4 + (f - 1))
                    w = slice(P * f, P * (f + 1))
                    for h in range(2):
                        r = slice(HS * h, HS * (h + 1))
                        T.matmul(ps[:, 2 + f % 2, r], w_hi[:, h, w], x_hi[:, r], start=True, stop=False)
                        T.matmul(ps[:, 2 + f % 2, r], w_hi[:, h, w], x_lo[:, r], start=False, stop=False)
                        ins = T.matmul(ps[:, 2 + f % 2, r], w_lo[:, h, w], x_hi[:, r], start=False, stop=True)
                    ins.then_inc(h_psum, 1)

                def result(n, f):
                    if f in POOL_TILES:
                        k = len(POOL_TILES)
                        pe.wait_ge(h_lo_pool, n * k + (POOL_TILES.index(f) + 1))
                    else:
                        k = FT - len(POOL_TILES)
                        pe.wait_ge(h_lo_ready, n * k + (f - sum(g < f for g in POOL_TILES) + 1))
                    w = slice(FF + P * f, FF + P * (f + 1))
                    for h in range(2):
                        r = slice(HS * h, HS * (h + 1))
                        T.matmul(ps[:, 2, r], w_hi[:, h, w], h_hi[:, f, r], start=(f == 0 and h == 0), stop=False)
                        T.matmul(ps[:, 2, r], w_hi[:, h, w], h_lo[:, f, r], start=False, stop=False)
                        ins = T.matmul(ps[:, 2, r], w_lo[:, h, w], h_hi[:, f, r], start=False,
                                       stop=(f == FT - 1 and h == 1))
                    if f == FT - 1:
                        ins.then_inc(y_psum, 1)

                def operands():
                    if (st + 1) % 2 == 0:
                        pe.wait_ge(k_in[(st + 1) // 2 % 2], (batch(1) + 1) * ROWS_IN)
                    pe.wait_ge(q_in[(st + 1) % 4], (batch(1) + 1) * ROWS_IN)

                def turn_maxima():
                    pe.wait_ge(max_ready, (t + 1) * 16)
                    if o_on:
                        pe.wait_ge(att_ready, t - 1)
                    T.transpose(ps[0:16, 7, 0:P], neg_max[:, st % 2, :], ident).then_inc(mt_psum, 1)

                def score(c, k):
                    if no_block(st):
                        if c < 3 and s_on:
                            scores(st, t, (4 + 4 * c + k,))
                        if c == 3 and b_on:
                            scores(st + 1, t + 1, (k,))
                    elif s_on and k < 3:
                        scores(st, t, (4 + 3 * c + k,))

                def output():
                    pe.wait_ge(pv_copied, t - 1)
                    if has_unit(st - 1):
                        pe.wait_ge(m_ready, t)
                    else:
                        pe.wait_ge(att_ready, t - 2)
                    for q in range(TPB):
                        ins = T.transpose(ps[:, 7, P * q:P * (q + 1)], pv_sb[:, P * q:P * (q + 1)], ident)
                    ins.then_inc(o_psum, 1)

                def probability(c, j):
                    if a_on:
                        probabilities(st - 1, t - 1, c, (j,))

                if no_block(st):
                    for c in range(3):
                        score(c, 0)
                        if c == 0:
                            score(c, 1)
                            if a_on:
                                pe.wait_ge(m_rows, t * 32)
                        probability(c, 0)
                        probability(c, 1)
                        if c >= 1:
                            score(c, 1)
                        if c == 1 and o_on:
                            output()
                        probability(c, 2)
                        score(c, 2)
                        if a_on and c >= 1:
                            sums(st - 1, t - 1, c - 1, half(1))
                        score(c, 3)
                        probability(c, 3)
                    if b_on:
                        operands()
                    score(3, 0)
                    probability(3, 0)
                    if s_on:
                        turn_maxima()
                    probability(3, 1)
                    score(3, 1)
                    probability(3, 2)
                    probability(3, 3)
                    if a_on:
                        sums(st - 1, t - 1, 2, None)
                    score(3, 2)
                    score(3, 3)
                    if a_on:
                        sums(st - 1, t - 1, 3, None)
                    return

                if a_on:
                    pe.wait_ge(m_rows, t * 32)
                for c in range(4):
                    probability(c, 0)
                    score(c, 0)
                    probability(c, 1)
                    if c == 0 and y_on:
                        result(n - 1, 1)
                        result(n - 1, 2)
                    if c == 1 and o_on:
                        output()
                    if c == 2 and f_on:
                        pe.wait_ge(block_in[(st - FIRST_BLOCK) % 2], half(2 - FIRST_BLOCK) * BLOCK_IN)
                        if st > FIRST_BLOCK:
                            pe.wait_ge(y_copied, n)
                        for q in range(4):
                            ins = T.transpose(ps[:, 2, P * q:P * (q + 1)], x_rows[:, (st - FIRST_BLOCK) % 2, q, 0:DM], ident)
                        ins.then_inc(xt_psum, 1)
                    if c == 2 and y_on:
                        pe.wait_ge(y_copied, n)
                        for q in range(4):
                            ins = T.transpose(ps[:, 3, P * q:P * (q + 1)], y_sb[:, P * q:P * (q + 1)], ident)
                        ins.then_inc(yt_psum, 1)
                    if a_on and c == 3:
                        sums(st - 1, t - 1, c - 1, None)
                    probability(c, 2)
                    score(c, 1)
                    probability(c, 3)
                    score(c, 2)
                    if c == 0 and y_on:
                        result(n - 1, 3)
                    if a_on and 1 <= c < 3:
                        sums(st - 1, t - 1, c - 1, half(1))

                if b_on:
                    operands()
                if f_on:
                    pe.wait_ge(w_split, n * 2 + 1)
                    pe.wait_ge(x_lo_ready, n + 1)
                    if st > FIRST_BLOCK:
                        pe.wait_ge(yt_ready, n)
                    hidden(0)
                if b_on:
                    scores(st + 1, t + 1, (0,))
                if s_on:
                    turn_maxima()
                if b_on:
                    scores(st + 1, t + 1, (1,))
                if f_on:
                    hidden(1)
                if a_on:
                    sums(st - 1, t - 1, 3, None)
                if f_on:
                    hidden(2)
                if b_on:
                    scores(st + 1, t + 1, (2,))
                if f_on:
                    hidden(3)
                if b_on:
                    scores(st + 1, t + 1, (3,))
                if f_on:
                    pe.wait_ge(h_ready, n * 4 + 3)
                    pe.wait_ge(w_split, n * 2 + 2)
                    result(n, 0)

            pe.wait_ge(mem_used, BATCH)
            pe.wait_ge(k_in[0], ROWS_IN)
            pe.wait_ge(q_in[0], ROWS_IN)
            scores(0, 0, range(4))
            unit_loop(pe, step)


def kernel(**inputs):
    import concourse.bacc as bacc
    from concourse.bass_utils import run_bass_kernel_spmd

    a = {k[3:]: np.ascontiguousarray(v) for k, v in inputs.items()}
    f32 = a["attn_x"].dtype
    by_unit = np.arange(DM).reshape(2, 4, 2, DH).transpose(0, 2, 1, 3).reshape(DM)
    half = by_unit[:DM // 2]
    wv_router = np.zeros((DM, VCOLS + EXPERTS), f32)
    for kv in range(KVH):
        wv_router[:, kv * VW:kv * VW + DH] = a["attn_Wv"][:, kv * DH:(kv + 1) * DH]
    wv_router[:, VCOLS:] = a["ffn_router_w"].T
    mem_block = np.zeros((DM, 2 * MEMW), f32)
    for g in range(2):
        mem_block[64 * g:64 * g + 64, MEMW * g:MEMW * g + 64] = a["attn_memory"][half]
        mem_block[64 * g:64 * g + 64, MEMW * g + 64] = a["attn_memory_norm"][half]
    row = np.arange(P) % 32
    consts = np.zeros((P, C_ALL), f32)
    consts[:, C_IDENT:C_IDENT + P] = np.eye(P)
    consts[:, C_BELOW:C_BELOW + P] = np.triu(np.ones((P, P)), 1)
    consts[:, C_ONES:C_ONES + P] = 1.0
    consts[:, C_IOTA:C_IOTA + EXPERTS] = np.arange(EXPERTS)
    consts[:, C_FILL:C_FILL + FILLS] = HS * np.arange(FILLS)
    consts[:, C_HALF:C_HALF + 2 * BLOCKS] = np.arange(2 * BLOCKS)
    consts[:, C_NEXT:C_NEXT + EXPERTS * TILES] = np.arange(EXPERTS * TILES) % TILES > 0
    consts[(row == 24) | (row == 25), C_KONE] = 1.0
    w_experts = np.zeros((EXPERTS, P, 2 * FF), f32)
    w_experts[:, :, 0:FF] = a["ffn_w1"].transpose(0, 2, 1)
    w_experts[:, :, FF:] = a["ffn_w2"].reshape(EXPERTS, DM, FT, P).transpose(0, 3, 2, 1).reshape(EXPERTS, P, FF)
    b_experts = np.zeros((EXPERTS, P, FT + 1), f32)
    b_experts[:, :, 0:FT] = a["ffn_b1"].reshape(EXPERTS, FT, P).transpose(0, 2, 1)
    b_experts[:, :, FT] = a["ffn_b2"]
    arrays = {
        "x": a["attn_x"],
        "wq": np.ascontiguousarray(a["attn_Wq"][:, by_unit]),
        "wk": a["attn_Wk"],
        "wv_router": wv_router,
        "mem_block": mem_block,
        "mem_weight": a["attn_memory_weight"],
        "w_experts": w_experts,
        "b_experts": b_experts,
        "consts": consts,
    }
    nc = bacc.Bacc("TRN2", target_bir_lowering=False, num_devices=1)
    args = [nc.dram_tensor(f"in_{k}", v.shape, mybir.dt.from_np(v.dtype), kind="ExternalInput").ap()
            for k, v in arrays.items()]
    out = nc.dram_tensor("out", arrays["x"].shape, F32, kind="ExternalOutput").ap()
    build(nc, *args, out)
    r = run_bass_kernel_spmd(nc, [{f"in_{k}": v for k, v in arrays.items()}], core_ids=[0])
    return r.results[0]["out"]
```
